# Optimizing a Trainium2 kernel written in Bass

```python
import numpy as np
import jax
import jax.numpy as jnp

def _softmax(x, axis=-1):
    return jax.nn.softmax(x, axis=axis)

def _gelu(x):
    return jax.nn.gelu(x, approximate=True)

def _silu(x):
    return jax.nn.silu(x)

def _sigmoid(x):
    return jax.nn.sigmoid(x)

def _layernorm(x, axis=-1, eps=1e-05):
    m = jnp.mean(x, axis=axis, keepdims=True)
    v = jnp.var(x, axis=axis, keepdims=True)
    return (x - m) / jnp.sqrt(v + eps)

def _scatter_add(tgt, idx, src, axis=0):
    return tgt.at[idx].add(src)

def _segment_sum(src, seg, n):
    return jax.ops.segment_sum(src, seg, n)
kernel_name = 'mk_flamingo_gated_d1_seqx_r8_8afc83'

def setup_inputs(seed: int=0):
    np.random.seed(seed)
    _w = jnp.asarray

    def _rec_inputs():
        import jax
        import jax.numpy as jnp
        _rk = jax.random.key(seed)
        x = -0.0002928 + 1 * jax.random.normal(jax.random.fold_in(_rk, 1), (32, 56, 128), jnp.float32)
        _lenS = 56 - jax.random.randint(jax.random.fold_in(_rk, 7), (32,), 0, max(1, 56 // 4) + 1, jnp.int32)
        _lenS2 = 1500 - jax.random.randint(jax.random.fold_in(_rk, 8), (32,), 0, max(1, 1500 // 4) + 1, jnp.int32)
        _ctx_1024P = jax.random.normal(jax.random.fold_in(_rk, 11), (32, 16, 128), jnp.float32)
        _ctx_1024c = jax.random.dirichlet(jax.random.fold_in(_rk, 511), 0.3 * jnp.ones((16,), jnp.float32), (32, 1500))
        _ctx_1024t = jnp.einsum('bsk,bkd->bsd', _ctx_1024c, _ctx_1024P)
        _ctx_1024t = _ctx_1024t * jax.lax.rsqrt(jnp.mean(jnp.square(_ctx_1024t)) + 1e-12) * 0.953939
        ctx_1024 = -0.000191848 + 0.999787 * (_ctx_1024t + 0.3 * jax.random.normal(jax.random.fold_in(_rk, 611), (32, 1500, 128), jnp.float32))
        _g = jax.random.normal(jax.random.fold_in(_rk, 9001), (2, 1), jnp.float32)
        _g = jnp.sign(_g) * jnp.maximum(jnp.abs(_g), 1.0) + (_g == 0) * 1.0
        g_xattn = _g[0]
        g_ffn = _g[1]
        return (x, ctx_1024, g_xattn, g_ffn)
    x, ctx_1024, g_xattn, g_ffn = _rec_inputs()

    def _L0_xattn_setup():
        import jax, jax.numpy as jnp
        import numpy as np
        D_MODEL = 128
        NUM_HEADS = 16
        DEPTH = D_MODEL // NUM_HEADS
        key = jax.random.key(seed)
        ks = jax.random.split(key, 10)
        B, T, C = (2, 256, 384)
        s = 1.0 / np.sqrt(D_MODEL)
        inp = {'x': jax.random.normal(ks[0], (B, T, D_MODEL), dtype=jnp.float32), 'context': jax.random.normal(ks[1], (B, C, D_MODEL), dtype=jnp.float32), 'Wq': jax.random.normal(ks[2], (D_MODEL, D_MODEL), dtype=jnp.float32) * s, 'bq': jnp.zeros((D_MODEL,), dtype=jnp.float32), 'Wk': jax.random.normal(ks[3], (D_MODEL, D_MODEL), dtype=jnp.float32) * s, 'bk': jnp.zeros((D_MODEL,), dtype=jnp.float32), 'Wv': jax.random.normal(ks[4], (D_MODEL, D_MODEL), dtype=jnp.float32) * s, 'bv': jnp.zeros((D_MODEL,), dtype=jnp.float32), 'Wo': jax.random.normal(ks[5], (D_MODEL, D_MODEL), dtype=jnp.float32) * s, 'bo': jnp.zeros((D_MODEL,), dtype=jnp.float32)}
        return inp
    _L0_xattn_all = _L0_xattn_setup()
    _L0_xattn_in = {k: v for k, v in _L0_xattn_all.items() if k in ('Wq', 'bq', 'Wk', 'bk', 'Wv', 'bv', 'Wo', 'bo')}
    del _L0_xattn_all

    def _L0_ffn_setup():
        import jax, jax.numpy as jnp
        import numpy as np
        NUM_EXPERTS = 160
        TOP_K = 8
        ROUTED_SCALE = 2.5
        HIDDEN = 128
        INTER = 64
        key = jax.random.key(seed)
        ks = jax.random.split(key, 7)
        B, S = (1, 256)
        return {'hidden_states': jax.random.normal(ks[0], (B, S, HIDDEN), dtype=jnp.float32), 'router_w': jax.random.normal(ks[1], (NUM_EXPERTS, HIDDEN), dtype=jnp.float32) * 0.02, 'expert_bias': jnp.zeros((NUM_EXPERTS,), dtype=jnp.float32), 'w_gate': jax.random.normal(ks[2], (NUM_EXPERTS, INTER, HIDDEN), dtype=jnp.float32) * 0.02, 'w_down': jax.random.normal(ks[3], (NUM_EXPERTS, HIDDEN, INTER), dtype=jnp.float32) * 0.02, 'w_gate_shared': jax.random.normal(ks[4], (INTER, HIDDEN), dtype=jnp.float32) * 0.02, 'w_down_shared': jax.random.normal(ks[5], (HIDDEN, INTER), dtype=jnp.float32) * 0.02}
    _L0_ffn_all = _L0_ffn_setup()
    _L0_ffn_in = {k: v for k, v in _L0_ffn_all.items() if k in ('router_w', 'expert_bias', 'w_gate', 'w_down', 'w_gate_shared', 'w_down_shared')}
    del _L0_ffn_all
    return {'x': x, 'ctx_1024': ctx_1024, 'g_xattn': g_xattn, 'g_ffn': g_ffn, 'L0_xattn_Wq': _L0_xattn_in['Wq'], 'L0_xattn_bq': _L0_xattn_in['bq'], 'L0_xattn_Wk': _L0_xattn_in['Wk'], 'L0_xattn_bk': _L0_xattn_in['bk'], 'L0_xattn_Wv': _L0_xattn_in['Wv'], 'L0_xattn_bv': _L0_xattn_in['bv'], 'L0_xattn_Wo': _L0_xattn_in['Wo'], 'L0_xattn_bo': _L0_xattn_in['bo'], 'L0_ffn_router_w': _L0_ffn_in['router_w'], 'L0_ffn_expert_bias': _L0_ffn_in['expert_bias'], 'L0_ffn_w_gate': _L0_ffn_in['w_gate'], 'L0_ffn_w_down': _L0_ffn_in['w_down'], 'L0_ffn_w_gate_shared': _L0_ffn_in['w_gate_shared'], 'L0_ffn_w_down_shared': _L0_ffn_in['w_down_shared']}

def reference(x, ctx_1024, g_xattn, g_ffn, L0_xattn_Wq, L0_xattn_bq, L0_xattn_Wk, L0_xattn_bk, L0_xattn_Wv, L0_xattn_bv, L0_xattn_Wo, L0_xattn_bo, L0_ffn_router_w, L0_ffn_expert_bias, L0_ffn_w_gate, L0_ffn_w_down, L0_ffn_w_gate_shared, L0_ffn_w_down_shared):
    import jax
    import jax.numpy as jnp

    def _L0_xattn_ref(x, context, Wq, bq, Wk, bk, Wv, bv, Wo, bo):
        import jax, jax.numpy as jnp
        import numpy as np
        D_MODEL = 128
        NUM_HEADS = 16
        DEPTH = D_MODEL // NUM_HEADS
        B, T, D = x.shape
        C = context.shape[1]
        H, d = (NUM_HEADS, DEPTH)
        q = x @ Wq.T + bq
        k = context @ Wk.T + bk
        v = context @ Wv.T + bv
        q = q.reshape(B, T, H, d).transpose(0, 2, 1, 3)
        k = k.reshape(B, C, H, d).transpose(0, 2, 1, 3)
        v = v.reshape(B, C, H, d).transpose(0, 2, 1, 3)
        scores = jnp.einsum('bhtd,bhcd->bhtc', q, k) / jnp.sqrt(jnp.asarray(d, x.dtype))
        attn = jax.nn.softmax(scores, axis=-1)
        out = jnp.einsum('bhtc,bhcd->bhtd', attn, v)
        out = out.transpose(0, 2, 1, 3).reshape(B, T, D)
        return out @ Wo.T + bo

    def _L0_ffn_ref(hidden_states, router_w, expert_bias, w_gate, w_down, w_gate_shared, w_down_shared):
        import jax, jax.numpy as jnp
        import numpy as np
        NUM_EXPERTS = 160
        TOP_K = 8
        ROUTED_SCALE = 2.5
        HIDDEN = 128
        INTER = 64
        B, S, H = hidden_states.shape
        x = hidden_states.reshape(-1, H)
        T = x.shape[0]
        logits = x @ router_w.T + expert_bias[None, :]
        probs = jax.nn.sigmoid(logits)
        top_w, top_idx = jax.lax.top_k(probs, TOP_K)
        top_w = top_w / (jnp.sum(top_w, axis=-1, keepdims=True) + 1e-09)
        top_w = top_w * ROUTED_SCALE
        combine = jnp.zeros((T, NUM_EXPERTS), dtype=x.dtype)
        combine = combine.at[jnp.arange(T)[:, None], top_idx].set(top_w)
        h1 = jax.nn.silu(jnp.einsum('th,eih->eti', x, w_gate))
        h1w = h1 * combine.T[:, :, None]
        routed = jnp.einsum('eti,ehi->th', h1w, w_down)
        shared = jax.nn.silu(x @ w_gate_shared.T) @ w_down_shared.T
        return (routed + shared).reshape(B, S, H)
    x = x + jnp.tanh(g_xattn[0]) * _L0_xattn_ref(_layernorm(x, axis=-1), ctx_1024, L0_xattn_Wq, L0_xattn_bq, L0_xattn_Wk, L0_xattn_bk, L0_xattn_Wv, L0_xattn_bv, L0_xattn_Wo, L0_xattn_bo)
    x = x + jnp.tanh(g_ffn[0]) * _L0_ffn_ref(_layernorm(x, axis=-1), L0_ffn_router_w, L0_ffn_expert_bias, L0_ffn_w_gate, L0_ffn_w_down, L0_ffn_w_gate_shared, L0_ffn_w_down_shared)
    return x

_drawn_inputs = setup_inputs


def setup_inputs(seed=0):
    import zlib

    import numpy as np

    out = dict(_drawn_inputs(seed))
    spreads = {'L0_xattn_bq': (0.0, 0.445),
     'L0_xattn_bk': (0.0, 0.8),
     'L0_xattn_bv': (0.0, 0.1),
     'L0_xattn_bo': (0.0, 0.1),
     'L0_ffn_expert_bias': (0.0, 0.666)}
    factors = {'L0_ffn_router_w': 4.207,
     'L0_ffn_w_gate': 4.031,
     'L0_ffn_w_down': 4.01,
     'L0_ffn_w_gate_shared': 3.574,
     'L0_ffn_w_down_shared': 3.493}
    for name, (base, spread) in spreads.items():
        noise = np.random.default_rng([zlib.crc32(name.encode()), seed]).standard_normal(out[name].shape)
        drawn = base * np.exp(spread * noise) if base else spread * noise
        out[name] = jnp.asarray(drawn.astype(out[name].dtype))
    for name, factor in factors.items():
        out[name] = (out[name] * factor).astype(out[name].dtype)
    return out
```

```python
import concourse.bass as bass
from concourse import mybir
from contextlib import ExitStack


def flamingo_gated_block(nc, x, ctx, g_xattn, g_ffn, Wq, bq, Wk, bk, Wv, bv, Wo, bo,
                         router_w, expert_bias, w_gate, w_down, w_gate_shared, w_down_shared, out):
    fp32 = mybir.dt.float32
    fp16 = mybir.dt.float16
    bf16 = mybir.dt.bfloat16
    ALU = mybir.AluOpType
    ACT = mybir.ActivationFunctionType
    AX = mybir.AxisListType

    B, T, D = x.shape
    C = ctx.shape[1]
    H = 16
    d = D // H
    E, I, _ = w_gate.shape
    TOP_K = 8
    ROUTED_SCALE = 2.5
    EPS_LN = 1e-5
    EPS_TOPK = 1e-9
    QSCALE = float(d) ** -0.5

    N = B * T
    PT = 2 * T
    NP = B // 2
    HT = H * T
    KT = 12
    KP = C // KT
    NCH = 3
    CK = C // NCH
    TPC = KT // NCH
    MT = HT // 128
    HG = 4
    GC = HT // HG
    VG = 6
    VC = 3 * T
    PR = 3
    NTC = 4
    TC = N // NTC
    PPC = NP // NTC
    EG = 4
    GE = E // EG
    EP = E // 2
    GP = GE // 2
    WPP = EP // (B // 2)
    WR = 4
    LAG = 2
    PREP_AT = {0: [(1, 0), (3, 1), (7, 2)], 1: [(1, 3), (7, 4)]}
    DEN_AT, OUT_AT, NEG_AT = 5, 9, KT - 1

    stk = ExitStack()
    with stk:
        def sb(name, shape, dt=fp32):
            return stk.enter_context(nc.sbuf_tensor(name, shape, dt))

        def sem(name):
            return stk.enter_context(nc.semaphore(name))

        ident = sb("ident", [128, 128])
        ident16 = sb("ident16", [128, 128], fp16)
        identb = sb("identb", [128, 128], bf16)
        head_mask = sb("head_mask", [128, H], fp16)
        stack_mask = sb("stack_mask", [128, HG], fp16)
        den_pick = sb("den_pick", [128, 128])
        expand = sb("expand", [128, GE, I], bf16)
        ones_d = sb("ones_d", [D, PT])
        w_raw = sb("w_raw", [128, 4, D])
        wqT = sb("wqT", [D, D])
        woT = sb("woT", [D, D])
        wk_hi = sb("wk_hi", [D, D], fp16)
        wk_lo = sb("wk_lo", [D, D], fp16)
        wv_hi = sb("wv_hi", [D, D], fp16)
        wv_lo = sb("wv_lo", [D, D], fp16)
        wo_m = sb("wo_m", [128, 2, 3, D])
        bqc = sb("bqc", [D, 1])
        bqs = sb("bqs", [D, 1])
        bkc = sb("bkc", [D, 1])
        bvc = sb("bvc", [D, 1])
        bv_rep = sb("bv_rep", [D, PT])
        bo_b = sb("bo_b", [PT, D])
        eb_b = sb("eb_b", [PT, E])
        g_raw = sb("g_raw", [PT, 2])
        tg = sb("tg", [PT, 2])
        xt = sb("xt", [PT, NP, D])
        xc = sb("xc", [PT, NP, D])
        stat = sb("stat", [PT, 5, NP])
        xnT = sb("xnT", [D, N])
        q_hi = sb("q_hi", [D, N], fp16)
        q_lo = sb("q_lo", [D, N], fp16)
        q_stk = sb("q_stk", [128, HG, N], fp16)
        ctx_in = sb("ctx_in", [KP, 2, KT, D])
        ctT = sb("ctT", [D, 2, 2, C], fp16)
        kparts = sb("kparts", [D, 2, 2, C], fp16)
        k_stk = sb("k_stk", [128, 2, HG, C], fp16)
        v_sb = sb("v_sb", [KP, 2, KT, VG, 32])
        q_blk = sb("q_blk", [D, 2, H, T], fp16)
        q_st = sb("q_st", [128, 2, HG, HG, T], fp16)
        part_max = sb("part_max", [128, MT, NCH])
        neg_max = sb("neg_max", [128, MT], fp16)
        neg_row = sb("neg_row", [MT, 128], fp16)
        p_exp = sb("p_exp", [KP, PR, HT])
        o_raw = sb("o_raw", [128, 2 * VC])
        o_rec = sb("o_rec", [128, 2 * VC])
        o_nrm = sb("o_nrm", [128, 6, 2, T])
        w_in = sb("w_in", [128, WPP, 2, 128])
        w_out = sb("w_out", [128, WPP, 4, 128], fp16)
        w_ring = sb("w_ring", [128, WR, 4, 128], fp16)
        sh_raw = sb("sh_raw", [128, 2, D])
        sg = sb("sg", [128, 2, I], fp16)
        sd = sb("sd", [I, 2, D], fp16)
        r_raw = sb("r_raw", [E // 2, 2, D])
        rT = sb("rT", [D, E])
        top = sb("top", [PT, NP, TOP_K])
        wsum = sb("wsum", [PT, 3, NP])
        w_scratch = nc.dram_tensor("w_scratch", [EP, 128, 4, 128], fp16, kind="Internal").ap()

        def flat(ap, pattern, dt=None):
            a = ap.rearrange(pattern)
            return a.bitcast(dt) if dt is not None else a

        k_words = flat(kparts[:, :, :, :], "p a b c -> p (a b c)", fp32)
        sq = k_words[0:PT, 0:NP * D].rearrange("p (n c) -> p n c", c=D)
        q_tmp = k_words[:, 0:TC]
        s_act = k_words[:, 0:2 * TC].rearrange("p (a t) -> p a t", a=2)
        prob = flat(p_exp[0:PT, :, :], "p a b -> p (a b)")[:, 0:NP * E].rearrange("p (n e) -> p n e", e=E)
        c_words = flat(ctx_in[:, :, :, :], "p a b c -> p (a b c)")
        rep = c_words[0:PT, 0:NP * E].rearrange("p (n e) -> p n e", e=E)
        comb = flat(v_sb[0:PT, :, :, :, :], "p a b c e -> p (a b c e)")[:, 0:NP * E].rearrange("p (n e) -> p n e", e=E)
        PW = 3 * GE
        parts = flat(k_stk[0:PT, :, :, :], "p a b c -> p (a b c)", bf16)[:, 0:NP * EG * PW]\
            .rearrange("p (n g w) -> p n g w", g=EG, w=PW)
        combT = q_stk[:, :, :].bitcast(bf16)
        h_words = flat(k_stk[:, :, :, :], "p a b c -> p (a b c)", fp32)
        h_f = h_words[:, 0:NTC * TC].rearrange("p (a t) -> p a t", a=NTC)
        t_words = flat(ctT[:, :, :, :], "p a b c -> p (a b c)")
        h_hi = t_words[:, 0:NTC * TC].rearrange("p (a t) -> p a t", a=NTC)
        h_lo = t_words[:, NTC * TC:2 * NTC * TC].rearrange("p (a t) -> p a t", a=NTC)

        bank = [stk.enter_context(nc.psum_tensor(f"bank{i}", [128, 512], fp32)) for i in range(8)]
        ST = [bank[0], bank[1]]
        SM = [bank[2], bank[3]]
        OB = bank[4]
        PJ = [bank[5], bank[6]]
        EB = bank[7]
        YB = [bank[0], bank[1], bank[2], bank[3]]
        ZB = [bank[4], bank[5]]
        CB = [bank[6], bank[7]]

        names = """consts small_in x_in wp_tr wp_cp wp_lo ln_sub ln_sq ln_var ln_root ln_done xn_tr xn_cp gates
            q_mm q_hi_done q_lo_done q_rows wo_rows cv_mm pre_done sh_tr sh_cp sh_lo o_cleared
            t_done ct_hi ct_lo kp_done k_hi_done k_lo_done vp_done v_copied qblk_made qst_made
            sm_done sm_maxed neg_made neg_tr neg_copied st_done exp_done pv_done o_copied den_done rec_done
            nrm_done op_done x2_done w_tr w_hi_done w_lo_done
            xf_cp xh_cp xl_cp lg_mm lg_biased prob_done top_done comb_done part_cast part_rest parts_done cb_tr cb_cp
            z_done c_done s_done h_done hh_done hl_done dn_done y_cp y_tr fin_done stored dve_chain""".split()
        S = {name: sem(name) for name in names}
        (consts, small_in, x_in, wp_tr, wp_cp, wp_lo, ln_sub, ln_sq, ln_var, ln_root, ln_done, xn_tr, xn_cp, gates,
         q_mm, q_hi_done, q_lo_done, q_rows, wo_rows, cv_mm, pre_done, sh_tr, sh_cp, sh_lo, o_cleared,
         t_done, ct_hi, ct_lo, kp_done, k_hi_done, k_lo_done, vp_done, v_copied, qblk_made, qst_made,
         sm_done, sm_maxed, neg_made, neg_tr, neg_copied, st_done, exp_done, pv_done, o_copied, den_done, rec_done,
         nrm_done, op_done, x2_done, w_tr, w_hi_done, w_lo_done,
         xf_cp, xh_cp, xl_cp, lg_mm, lg_biased, prob_done, top_done, comb_done, part_cast, part_rest, parts_done, cb_tr, cb_cp,
         z_done, c_done, s_done, h_done, hh_done, hl_done, dn_done, y_cp, y_tr, fin_done, stored, dve_chain) = \
            [S[name] for name in names]
        ctx_here = [sem(f"ctx_here{i}") for i in range(2)]
        kst_here = [sem(f"kst_here{i}") for i in range(2)]
        row_here = [sem(f"row_here{i}") for i in range(2)]
        w_here = [sem(f"w_here{i}") for i in range(WPP)]
        w_stored = [sem(f"w_stored{i}") for i in range(WPP)]
        ring_here = [sem(f"ring_here{i}") for i in range(WR)]
        NCONST = 22
        NSMALL = 14

        def back(hu, n):
            v = hu[1] - n
            return (hu[0] + v // 2, v % 2)

        def num(hu):
            return hu[0] * 2 + hu[1]

        def on(step, n):
            return not isinstance(step[0], int) or 0 <= num(step) - n < B

        def until(eng, s, value):
            if not isinstance(value, int) or value > 0:
                eng.wait_ge(s, value)

        def attention(eng, body, loop_to=B):
            for s in range(4):
                body((s // 2, s % 2))
            with eng.Fori(2, loop_to // 2) as h:
                body((h, 0))
                body((h, 1))
            for s in range(loop_to, B + 3):
                body((s // 2, s % 2))

        def tile_at(step, k, late):
            j = k - LAG - late
            return (j, back(step, 2), on(step, 2)) if j >= 0 else (j + KT, back(step, 3), on(step, 3))

        def pj(step, kind, c):
            return PJ[(step[1] + 3 * c + "TKV".index(kind)) % 2]

        def row(ap):
            return ap.rearrange("(a n) -> a n", a=1)

        x_pairs = x.rearrange("(n b) t c -> (b t) n c", b=2)
        out_pairs = out.rearrange("(n b) t c -> (b t) n c", b=2)
        gate_pairs = w_gate.rearrange("(n e) i h -> n (e i) h", e=2)
        down_pairs = w_down.rearrange("(n e) h i -> n h e i", e=2)

        block = stk.enter_context(nc.Block())

        @block.sync
        def _(sp):
            sp.dma_start(xt[0:T, :, :], x.rearrange("(n b) t c -> b t n c", b=2)[0]).then_inc(x_in, 16)
            sp.dma_start(xt[T:PT, :, :], x.rearrange("(n b) t c -> b t n c", b=2)[1]).then_inc(x_in, 16)
            for n, w in enumerate((Wq, Wk, Wv, Wo)):
                sp.dma_start(w_raw[:, n, :], w).then_inc(small_in, 16)
            for dst, src in ((bqc, bq), (bkc, bk), (bvc, bv)):
                sp.dma_start(dst[:, :], src.rearrange("(p a) -> p a", a=1)).then_inc(small_in, 16)
            sp.dma_start(bo_b[:, :], row(bo).to_broadcast([PT, D])).then_inc(small_in, 16)
            sp.dma_start(eb_b[:, :], row(expert_bias).to_broadcast([PT, E])).then_inc(small_in, 16)
            for n, g in enumerate((g_xattn, g_ffn)):
                sp.dma_start(g_raw[:, n:n + 1], row(g).to_broadcast([PT, 1])).then_inc(small_in, 16)
            sp.dma_start(sh_raw[0:I, 0, :], w_gate_shared).then_inc(small_in, 16)
            sp.dma_start(sh_raw[:, 1, 0:I], w_down_shared).then_inc(small_in, 16)
            sp.dma_start(r_raw[:, :, :], router_w.rearrange("(a p) h -> p a h", a=2)).then_inc(small_in, 16)
            sp.dma_start(ctx_in[:, 0, :, :], ctx[0].rearrange("(p j) c -> p j c", j=KT)).then_inc(ctx_here[0], 16)
            sp.dma_start(ctx_in[:, 1, :, :], ctx[1].rearrange("(p j) c -> p j c", j=KT)).then_inc(ctx_here[1], 16)
            sp.wait_ge(wp_cp, 4)
            sp.wait_ge(o_cleared, 1)
            for h in range(H):
                g, c = h // 3, h % 3
                p0 = 32 * (g % 4) + d * c
                sp.dma_start(wo_m[p0:p0 + d, g // 4, c, :], woT[d * h:d * h + d, :]).then_inc(wo_rows, 16)
            sp.wait_ge(q_hi_done, NTC)
            sp.wait_ge(q_lo_done, NTC)
            for g in range(HG):
                for r, part in enumerate((q_hi, q_lo, q_hi)):
                    sp.dma_start(q_stk[32 * r:32 * r + 32, g, :], part[32 * g:32 * g + 32, :]).then_inc(q_rows, 16)

            def body(step):
                if on(step, 1):
                    h, u = back(step, 1)
                    b = num((h, u))
                    read, made = (b - 1) * (2 * KT), b * NCH + NCH
                    if not isinstance(h, int):
                        read, made = sp.to_reg(read), sp.to_reg(made)
                    until(sp, st_done, read)
                    sp.wait_ge(k_lo_done, made)
                    for g in range(HG):
                        for r, part in enumerate((0, 0, 1)):
                            sp.dma_start(k_stk[32 * r:32 * r + 32, u, g, :], kparts[32 * g:32 * g + 32, u, part, :])\
                              .then_inc(kst_here[u], 16)
                if on(step, -1) and not (isinstance(step[0], int) and num(step) < 1):
                    h, u = back(step, -1)
                    b = num((h, u))
                    sp.wait_ge(t_done, (b - 1) * NCH)
                    sp.dma_start(ctx_in[:, u, :, :], ctx[bass.ds(b, 1)].rearrange("a (p j) c -> p (a j) c", j=KT))\
                      .then_inc(ctx_here[u], 16)
                if on(step, 1):
                    u = back(step, 1)[1]
                    b = num(back(step, 1))
                    sp.wait_ge(qst_made, b + 1)
                    sp.wait_ge(neg_copied, b + 1)
                    sp.dma_start(q_st[96:97, u, :, :, :].rearrange("p a b c -> p (a b c)"), neg_row[:, :])\
                      .then_inc(row_here[u], 16)

            attention(sp, body, B - 2)

            for i in range(WPP):
                sp.wait_ge(w_stored[i], 16 * (B // 2))
            for n in range(WR):
                sp.dma_start(w_ring[:, n, :, :], w_scratch[n]).then_inc(ring_here[n], 16)
            with sp.Fori(1, EP // WR) as i:
                for q in range(WR):
                    sp.wait_ge(dn_done, i * (WR * NTC) + (q - WR + 2) * NTC)
                    sp.dma_start(w_ring[:, q, :, :], w_scratch[bass.ds(i * WR + q, 1)].rearrange("a p b c -> p (a b) c"))\
                      .then_inc(ring_here[q], 16)
            for c in range(NTC):
                sp.wait_ge(fin_done, c + 1)
                for b in range(2):
                    sp.dma_start(out.rearrange("(n b) t c -> b t n c", b=2)[b, :, c * PPC:(c + 1) * PPC, :],
                                 xc[b * T:(b + 1) * T, c * PPC:(c + 1) * PPC, :]).then_inc(stored, 16)
            sp.wait_ge(stored, 16 * 2 * NTC)

        @block.gpsimd
        def _(pool):
            made = [0]

            def const(ins):
                made[0] += 1
                ins.then_inc(consts, 1)
                pool.wait_ge(consts, made[0])

            const(pool.memset(ident[:, :], 0.0))
            const(pool.memset(head_mask[:, :], 1.0))
            const(pool.memset(den_pick[:, :], 0.0))
            const(pool.memset(expand[:, :, :], 0.0))
            const(pool.affine_select(out=ident[:, :], in_=ident[:, :], compare_op=ALU.not_equal, fill=1.0,
                                     base=0, pattern=[[-1, 128]], channel_multiplier=1))
            const(pool.affine_select(out=head_mask[:, :], in_=head_mask[:, :], compare_op=ALU.is_ge, fill=0.0,
                                     base=0, pattern=[[-d, H]], channel_multiplier=1))
            dp = den_pick[:, :].rearrange("p (a b) -> p a b", b=32)
            const(pool.affine_select(out=dp, in_=dp, compare_op=ALU.not_equal, fill=1.0,
                                     base=3 * d, pattern=[[32, 4], [0, 32]], channel_multiplier=-1))
            const(pool.affine_select(out=head_mask[:, :], in_=head_mask[:, :], compare_op=ALU.is_ge, fill=0.0,
                                     base=d - 1, pattern=[[d, H]], channel_multiplier=-1))
            for r in range(3):
                const(pool.affine_select(out=expand[:, :, :], in_=expand[:, :, :], compare_op=ALU.not_equal,
                                         fill=1.0, base=GE * r, pattern=[[1, GE], [0, I]], channel_multiplier=-1))
            const(pool.tensor_copy(ident16[:, :], ident[:, :]))
            const(pool.tensor_copy(identb[:, :], ident[:, :]))
            const(pool.memset(stack_mask[96:128, :], 0.0))
            for r in range(3):
                const(pool.tensor_copy(stack_mask[32 * r:32 * r + 32, :], head_mask[32 * r:32 * r + 32, 4 * r:4 * r + 4]))
            const(pool.memset(q_stk[96:128, :, :], 0.0))
            const(pool.memset(k_stk[96:128, :, :, :], 0.0))
            const(pool.memset(v_sb[:, :, :, :, :], 1.0))
            const(pool.memset(o_raw[:, :], 1.0))
            const(pool.memset(k_stk[96:97, :, :, :], 1.0))
            assert made[0] == NCONST

            def load_pair(step):
                for _, i in PREP_AT[step[1]]:
                    h = step[0]
                    until(pool, w_tr, h * WPP + (i + 1 - WPP))
                    pool.dma_start(w_in[:, i, 0, :], gate_pairs[bass.ds(h * WPP + i, 1)].rearrange("a p c -> p (a c)"))\
                        .then_inc(w_here[i], 16)
                    pool.dma_start(w_in[:, i, 1, :].rearrange("p (e c) -> p e c", e=2),
                                   down_pairs[bass.ds(h * WPP + i, 1)].rearrange("a h e c -> h (a e) c"))\
                        .then_inc(w_here[i], 16)

            def store_pair(step):
                for _, i in PREP_AT[step[1]]:
                    h = step[0]
                    pool.wait_ge(w_hi_done, h * WPP + (i + 1))
                    pool.wait_ge(w_lo_done, h * WPP + (i + 1))
                    pool.dma_start(w_scratch[bass.ds(h * WPP + i, 1)].rearrange("a p b c -> p (a b) c"), w_out[:, i, :, :])\
                        .then_inc(w_stored[i], 16)

            load_pair((0, 0))
            pool.wait_ge(q_rows, 16 * 3 * HG)
            pool.wait_ge(consts, NCONST)

            def body(step):
                if on(step, 0):
                    h, u = step
                    b = num(step)
                    until(pool, sm_done, (b - 1) * (MT * NCH))
                    pool.tensor_tensor(q_blk[:, u, :, :],
                                       q_hi[:, bass.ds(b * T, T)].unsqueeze(1).to_broadcast([D, H, T]),
                                       head_mask[:, :].unsqueeze(2).to_broadcast([D, H, T]), ALU.mult)\
                        .then_inc(qblk_made, 1)
                if on(step, 1):
                    store_pair(back(step, 1))
                if on(step, -1):
                    load_pair(back(step, -1))
                if on(step, 1):
                    h, u = back(step, 1)
                    b = num((h, u))
                    until(pool, st_done, (b - 1) * (2 * KT))
                    for g in range(HG):
                        last = pool.tensor_tensor(q_st[:, u, g, :, :],
                                                  q_stk[:, g, bass.ds(b * T, T)].unsqueeze(1).to_broadcast([128, HG, T]),
                                                  stack_mask[:, :].unsqueeze(2).to_broadcast([128, HG, T]), ALU.mult)
                    last.then_inc(qst_made, 1)

            attention(pool, body, B - 2)

        @block.scalar
        def _(act):
            for n, w in enumerate((wqT, wk_hi, wv_hi, woT)):
                act.wait_ge(wp_tr, n + 1)
                act.activation(w[:, :], bank[n][:, 0:D], ACT.Copy).then_inc(wp_cp, 1)
            act.wait_ge(small_in, 16 * NSMALL)
            act.activation(tg[:, :], g_raw[:, :], ACT.Tanh).then_inc(gates, 1)
            act.activation(bqs[:, :], bqc[:, :], ACT.Copy, scale=QSCALE).then_inc(gates, 1)

            def norm_act(n):
                act.wait_ge(ln_sub, n)
                act.activation(sq, xc[:, :, :], ACT.Square).then_inc(ln_sq, 1)
                act.wait_ge(ln_var, n)
                act.activation(stat[:, 3, :], stat[:, 2, :], ACT.Sqrt).then_inc(ln_root, 1)

            norm_act(1)
            for c in range(NTC):
                act.wait_ge(xn_tr, c + 1)
                act.activation(xnT[:, c * TC:(c + 1) * TC], bank[c][:, 0:TC], ACT.Copy).then_inc(xn_cp, 1)
            act.wait_ge(gates, 2)
            for c in range(NTC):
                act.wait_ge(q_mm, c + 1)
                act.activation(q_hi[:, c * TC:(c + 1) * TC], bank[4 + c][:, 0:TC], ACT.Identity,
                               bias=bqs[:, 0:1], scale=QSCALE).then_inc(q_hi_done, 1)
            act.wait_ge(sh_tr, 1)
            act.activation(sg[:, 0, :], bank[0][:, 0:I], ACT.Copy).then_inc(sh_cp, 1)
            act.wait_ge(sh_tr, 2)
            act.activation(sd[:, 0, :], bank[1][0:I, 0:D], ACT.Copy).then_inc(sh_cp, 1)
            act.wait_ge(sh_tr, 3)
            act.activation(rT[:, :], bank[2][:, 0:E], ACT.Copy).then_inc(sh_cp, 1)

            def body(step):
                for k in range(KT):
                    j, bt, there = tile_at(step, k, 0)
                    for f in range(2):
                        if there:
                            b = num(bt)
                            act.wait_ge(st_done, b * (2 * KT) + (2 * j + f + 1))
                            if f == 0:
                                until(act, pv_done, b * KT + (j - PR + 1))
                            act.activation(p_exp[:, j % PR, f * 448:(f + 1) * 448], ST[f][0:KP, 0:448],
                                           ACT.Exp).then_inc(exp_done, 1)
                        if f == 0:
                            evacuate(step, k - 1)

            def evacuate(step, k):
                if k < 0 and on(step, 2):
                    b = num(back(step, 2))
                    act.wait_ge(neg_tr, b + 1)
                    if not (isinstance(b, int) and b == 0):
                        hp, up = back(step, 3)
                        act.wait_ge(row_here[up], hp * 16 + 16)
                    act.activation(neg_row[:, :], EB[0:MT, 0:64].bitcast(fp16), ACT.Copy).then_inc(neg_copied, 1)
                if k >= 0 and on(step, 0):
                    h, u = step
                    b = num(step)
                    c = k // TPC
                    if k % TPC == 0:
                        act.wait_ge(t_done, b * NCH + (c + 1))
                        act.activation(ctT[:, u, 0, c * CK:(c + 1) * CK], pj(step, "T", c)[:, 0:CK],
                                       ACT.Copy).then_inc(ct_hi, 1)
                    if k % TPC == 2:
                        act.wait_ge(kp_done, b * NCH + (c + 1))
                        if c == 0:
                            until(act, sm_done, (b - 1) * (MT * NCH))
                            if not isinstance(h, int) or h > 0:
                                act.wait_ge(kst_here[u], h * (16 * 3 * HG))
                        act.activation(kparts[:, u, 0, c * CK:(c + 1) * CK], pj(step, "K", c)[:, 0:CK],
                                       ACT.Identity, bias=bkc[:, 0:1]).then_inc(k_hi_done, 1)
                    for at, i in PREP_AT[u]:
                        if at == k:
                            act.wait_ge(w_tr, h * WPP + (i + 1))
                            if not isinstance(h, int) or h > 0:
                                act.wait_ge(w_stored[i], h * 16)
                            act.activation(w_out[:, i, 0:4:2, :],
                                           EB[:, 0:256].rearrange("p (a b) -> p a b", a=2),
                                           ACT.Copy).then_inc(w_hi_done, 1)

            attention(act, body)

            norm_act(2)
            for c in range(NTC):
                act.wait_ge(xn_tr, NTC + c + 1)
                act.activation(q_hi[:, c * TC:(c + 1) * TC], bank[c][:, 0:TC], ACT.Copy).then_inc(xh_cp, 1)
            act.wait_ge(lg_biased, 6)
            act.activation(prob, prob, ACT.Sigmoid).then_inc(prob_done, 1)
            for r in range(2):
                act.wait_ge(comb_done if r == 0 else part_rest, 1)
                act.activation(parts[:, :, :, r * GE:(r + 1) * GE], comb.rearrange("p n (g e) -> p n g e", g=EG),
                               ACT.Copy).then_inc(part_cast, 1)
            for n in range(NP):
                act.wait_ge(cb_tr, n + 1)
                act.activation(combT[0:PW, :, n * PT:(n + 1) * PT],
                               bank[4 + n % 4][0:PW, 0:EG * PT // 2].bitcast(bf16).rearrange("p (g t) -> p g t", g=EG),
                               ACT.Copy).then_inc(cb_cp, 1)
            for t in range(NTC):
                act.wait_ge(z_done, t + 1)
                act.activation(h_f[0:I, t, :], ZB[t % 2][0:I, 0:TC], ACT.Silu).then_inc(s_done, 1)
                act.wait_ge(s_done, t + 1)
                act.activation(h_hi[0:I, t, :], h_f[0:I, t, :], ACT.Copy).then_inc(hh_done, 1)

            def silu(n, t, first=False):
                m = n * NTC + (NTC + t)
                act.wait_ge(z_done, m + 1)
                if not (first and t < 2):
                    act.wait_ge(h_done, m - (NTC + 1))
                act.activation(s_act[:, t % 2, :], ZB[t % 2][:, 0:TC], ACT.Silu).then_inc(s_done, 1)

            def hi_part(n, t):
                act.wait_ge(h_done, n * NTC + (t + 1))
                act.activation(h_hi[:, t, :], h_f[:, t, :], ACT.Copy).then_inc(hh_done, 1)

            def pairs(base, first=False):
                for q in range(WR):
                    for t in range(NTC):
                        f = first and q == 0
                        silu(base + q, t, f)
                        if t:
                            hi_part(base + q, t - 1)
                        elif not f:
                            hi_part(base + (q - 1), NTC - 1)

            pairs(0, True)
            with act.Fori(1, EP // WR) as i:
                pairs(i * WR)
            hi_part(EP - 1, NTC - 1)
            for c in range(NTC):
                act.wait_ge(dn_done, EP * NTC + NTC)
                act.activation(xnT[:, c * TC:(c + 1) * TC], YB[c][:, 0:TC], ACT.Copy).then_inc(y_cp, 1)

        @block.vector
        def _(dve):
            v = nc.vector
            chained = [0]

            def link(ins):
                chained[0] += 1
                ins.then_inc(dve_chain, 1)
                dve.wait_ge(dve_chain, chained[0])

            v.memset(wo_m[:, :, :, :], 0.0).then_inc(o_cleared, 1)
            v.memset(ones_d[:, :], 1.0).then_inc(o_cleared, 1)

            def norm(n):
                link(v.reduce_sum(stat[:, 0, :], xt[:, :, :], axis=AX.X))
                link(v.tensor_scalar(stat[:, 1, :], stat[:, 0, :], -1.0 / D, None, ALU.mult))
                v.tensor_tensor(xc[:, :, :], xt[:, :, :], stat[:, 1, :].unsqueeze(2).to_broadcast([PT, NP, D]),
                                ALU.add).then_inc(ln_sub, 1)
                dve.wait_ge(ln_sq, n)
                link(v.reduce_sum(stat[:, 0, :], sq, axis=AX.X))
                v.tensor_scalar(stat[:, 2, :], stat[:, 0, :], 1.0 / D, EPS_LN, ALU.mult, ALU.add).then_inc(ln_var, 1)
                dve.wait_ge(ln_root, n)
                link(v.reciprocal(stat[:, 4, :], stat[:, 3, :]))
                v.tensor_tensor(xc[:, :, :], xc[:, :, :], stat[:, 4, :].unsqueeze(2).to_broadcast([PT, NP, D]),
                                ALU.mult).then_inc(ln_done, 1)

            for n, (lo, hi) in enumerate(((wk_lo, wk_hi), (wv_lo, wv_hi))):
                dve.wait_ge(wp_cp, n + 2)
                v.tensor_tensor(lo[:, :], bank[n + 1][:, 0:D], hi[:, :], ALU.subtract).then_inc(wp_lo, 1)
            dve.wait_ge(x_in, 32)
            norm(1)
            dve.wait_ge(small_in, 16 * NSMALL)
            dve.wait_ge(o_cleared, 2)
            v.tensor_scalar(bv_rep[:, :], ones_d[:, :], bvc[:, 0:1], None, ALU.mult).then_inc(gates, 1)
            dve.wait_ge(gates, 2)
            for c in range(NTC):
                dve.wait_ge(q_hi_done, c + 1)
                if c:
                    dve.wait_ge(q_lo_done, c)
                link(v.tensor_scalar(q_tmp, bank[4 + c][:, 0:TC], QSCALE, bqs[:, 0:1], ALU.mult, ALU.add))
                v.tensor_tensor(q_lo[:, c * TC:(c + 1) * TC], q_tmp, q_hi[:, c * TC:(c + 1) * TC],
                                ALU.subtract).then_inc(q_lo_done, 1)
            dve.wait_ge(cv_mm, 1)
            link(v.tensor_tensor(bo_b[:, :], bank[3][0:PT, 0:D], bo_b[:, :], ALU.add))
            link(v.tensor_scalar(bo_b[:, :], bo_b[:, :], tg[:, 0:1], None, ALU.mult))
            v.tensor_tensor(xt[:, :, :], xt[:, :, :], bo_b[:, :].unsqueeze(1).to_broadcast([PT, NP, D]),
                            ALU.add).then_inc(pre_done, 1)
            dve.wait_ge(sh_cp, 2)
            v.tensor_tensor(sg[:, 1, :], bank[0][:, 0:I], sg[:, 0, :], ALU.subtract).then_inc(sh_lo, 1)
            v.tensor_tensor(sd[:, 1, :], bank[1][0:I, 0:D], sd[:, 0, :], ALU.subtract).then_inc(sh_lo, 1)
            dve.wait_ge(consts, NCONST)

            def maxima(step, i):
                b = num(back(step, 1))
                if i == 0:
                    until(dve, neg_made, b)
                dve.wait_ge(sm_done, b * (MT * NCH) + (i + 1))
                v.reduce_max(part_max[:, i // NCH, i % NCH:i % NCH + 1], SM[(back(step, 1)[1] + i) % 2][:, 0:CK],
                             axis=AX.X).then_inc(sm_maxed, 1)

            def body(step):
                for k in range(KT):
                    if on(step, 1) and 2 * k < MT * NCH:
                        maxima(step, 2 * k)
                    evacuate(step, k - 1)
                    if on(step, 3) and k == LAG:
                        b = num(back(step, 3))
                        dve.wait_ge(pv_done, b * KT + KT)
                        until(dve, nrm_done, b)
                        v.tensor_copy(o_raw[:, 0:VC], OB[:, 0:VC])
                        v.tensor_copy(o_raw[0:64, VC:VC + T], OB[0:64, VC:VC + T])
                        v.tensor_copy(o_raw[0:32, VC + T:2 * VC], OB[0:32, VC + T:2 * VC]).then_inc(o_copied, 1)
                    if on(step, 1) and 2 * k + 1 < MT * NCH:
                        maxima(step, 2 * k + 1)
                    if on(step, 3) and k - 1 == DEN_AT:
                        h, u = back(step, 3)
                        b = num((h, u))
                        v.reciprocal(o_rec[:, VC:2 * VC], EB[:, VC:2 * VC]).then_inc(rec_done, 1)
                        dve.wait_ge(rec_done, b * 2 + 2)
                        if u == 0:
                            until(dve, op_done, h)
                        v.tensor_tensor(o_nrm[:, :, u, :], o_raw[:, :].rearrange("p (n t) -> p n t", t=T),
                                        o_rec[:, :].rearrange("p (n t) -> p n t", t=T), ALU.mult).then_inc(nrm_done, 1)
                    if on(step, 1) and k == NEG_AT - 1:
                        b = num(back(step, 1))
                        dve.wait_ge(sm_maxed, b * (MT * NCH) + MT * NCH)
                        until(dve, neg_tr, b)
                        v.tensor_reduce(neg_max[:, :], part_max[:, :, :], axis=AX.X, op=ALU.max,
                                        negate=True).then_inc(neg_made, 1)

            def values(bt, bank_v, c):
                u = bt[1]
                b = num(bt)
                dve.wait_ge(vp_done, b * NCH + (c + 1))
                if c == 0:
                    until(dve, pv_done, (b - 1) * KT)
                src = bank_v[0:KP, :].rearrange("p (j n) -> p j n", n=D)
                v.tensor_copy(v_sb[:, u, c * TPC:(c + 1) * TPC, 0:5, 0:3 * d],
                              src[:, :, 0:15 * d].rearrange("p j (g n) -> p j g n", g=5))
                v.tensor_copy(v_sb[:, u, c * TPC:(c + 1) * TPC, 5, 0:d],
                              src[:, :, 15 * d:16 * d]).then_inc(v_copied, 1)

            def evacuate(step, k):
                c = k // TPC
                if k < 0 and on(step, 2):
                    values(back(step, 2), pj(back(step, 1), "V", NCH - 1), NCH - 1)
                if k < 0:
                    return
                if on(step, 0):
                    h, u = step
                    b = num(step)
                    if k % TPC == 0:
                        dve.wait_ge(ct_hi, b * NCH + (c + 1))
                        v.tensor_tensor(ctT[:, u, 1, c * CK:(c + 1) * CK], pj(step, "T", c)[:, 0:CK],
                                        ctT[:, u, 0, c * CK:(c + 1) * CK], ALU.subtract).then_inc(ct_lo, 1)
                    if k % TPC == 2:
                        dve.wait_ge(k_hi_done, b * NCH + (c + 1))
                        v.scalar_tensor_tensor(out=kparts[:, u, 1, c * CK:(c + 1) * CK],
                                               in0=pj(step, "K", c)[:, 0:CK], scalar=bkc[:, 0:1],
                                               in1=kparts[:, u, 0, c * CK:(c + 1) * CK],
                                               op0=ALU.add, op1=ALU.subtract).then_inc(k_lo_done, 1)
                    for at, i in PREP_AT[u]:
                        if at == k:
                            dve.wait_ge(w_hi_done, h * WPP + (i + 1))
                            v.tensor_tensor(w_out[:, i, 1:4:2, :], EB[:, 0:256].rearrange("p (a b) -> p a b", a=2),
                                            w_out[:, i, 0:4:2, :], ALU.subtract).then_inc(w_lo_done, 1)
                if on(step, 1) and k % TPC == 3:
                    values(back(step, 1), pj(step, "V", c), c)
                if on(step, 3) and k == DEN_AT:
                    b = num(back(step, 3))
                    dve.wait_ge(den_done, b + 1)
                    v.reciprocal(o_rec[:, 0:VC], EB[:, 0:VC]).then_inc(rec_done, 1)
                if on(step, 3) and k == OUT_AT and back(step, 3)[1] == 1:
                    h = back(step, 3)[0]
                    dve.wait_ge(op_done, h + 1)
                    v.scalar_tensor_tensor(out=xt[:, bass.ds(h, 1), :], in0=EB[0:PT, 0:D].unsqueeze(1),
                                           scalar=tg[:, 0:1], in1=xt[:, bass.ds(h, 1), :],
                                           op0=ALU.mult, op1=ALU.add).then_inc(x2_done, 1)

            attention(dve, body)

            dve.wait_ge(x2_done, NP)
            norm(2)
            for c in range(NTC):
                dve.wait_ge(xh_cp, c + 1)
                cols = slice(c * TC, (c + 1) * TC)
                v.tensor_copy(xnT[:, cols], bank[c][:, 0:TC]).then_inc(xf_cp, 1)
                v.tensor_tensor(q_lo[:, cols], bank[c][:, 0:TC], q_hi[:, cols], ALU.subtract).then_inc(xl_cp, 1)
            for q in range(6):
                n = min(3, NP - 3 * q)
                dve.wait_ge(lg_mm, q + 1)
                v.tensor_tensor(prob[:, 3 * q:3 * q + n, :],
                                bank[4 + q % 4][0:PT, 0:n * E].rearrange("p (n e) -> p n e", e=E),
                                eb_b[:, :].unsqueeze(1).to_broadcast([PT, n, E]), ALU.add).then_inc(lg_biased, 1)
            dve.wait_ge(prob_done, 1)
            for n in range(NP):
                v.max(top[:, n, :], prob[:, n, :]).then_inc(top_done, 1)
            for n in range(NP):
                dve.wait_ge(top_done, n + 1)
                v.match_replace(rep[:, n, :], top[:, n, :], prob[:, n, :], -1.0).then_inc(top_done, 1)
            link(v.reduce_sum(wsum[:, 0, :], top[:, :, :], axis=AX.X))
            link(v.tensor_scalar(wsum[:, 1, :], wsum[:, 0, :], EPS_TOPK, None, ALU.add))
            link(v.reciprocal(wsum[:, 2, :], wsum[:, 1, :]))
            dve.wait_ge(top_done, 2 * NP)
            link(v.scalar_tensor_tensor(out=comb, in0=rep, scalar=0.0, in1=prob, op0=ALU.is_lt, op1=ALU.mult))
            link(v.tensor_tensor(comb, comb, wsum[:, 2, :].unsqueeze(2).to_broadcast([PT, NP, E]), ALU.mult))
            v.tensor_scalar(comb, comb, ROUTED_SCALE, None, ALU.mult).then_inc(comb_done, 1)
            g4 = comb.rearrange("p n (g e) -> p n g e", g=EG)
            dve.wait_ge(part_cast, 1)
            v.tensor_tensor(g4, g4, parts[:, :, :, 0:GE], ALU.subtract).then_inc(part_rest, 1)
            dve.wait_ge(part_cast, 2)
            v.tensor_tensor(parts[:, :, :, 2 * GE:3 * GE], g4, parts[:, :, :, GE:2 * GE], ALU.subtract)\
                .then_inc(parts_done, 1)

            for t in range(NTC):
                dve.wait_ge(hh_done, t + 1)
                v.tensor_tensor(h_lo[0:I, t, :], h_f[0:I, t, :], h_hi[0:I, t, :], ALU.subtract).then_inc(hl_done, 1)

            def weigh(n, t, first=False):
                m = n * NTC + (NTC + t)
                dve.wait_ge(s_done, m + 1)
                dve.wait_ge(c_done, n * NTC + (t + 1))
                dve.wait_ge(hh_done, m - (NTC - 1))
                v.tensor_tensor(h_f[:, t, :], CB[t % 2][:, 0:TC], s_act[:, t % 2, :], ALU.mult).then_inc(h_done, 1)

            def lo_part(n, t):
                dve.wait_ge(hh_done, n * NTC + (NTC + t + 1))
                v.tensor_tensor(h_lo[:, t, :], h_f[:, t, :], h_hi[:, t, :], ALU.subtract).then_inc(hl_done, 1)

            def pairs(base, first=False):
                for q in range(WR):
                    for t in range(NTC):
                        weigh(base + q, t)
                        if t:
                            lo_part(base + q, t - 1)
                        elif not (first and q == 0):
                            lo_part(base + (q - 1), NTC - 1)

            pairs(0, True)
            with dve.Fori(1, EP // WR) as i:
                pairs(i * WR)
            lo_part(EP - 1, NTC - 1)
            for c in range(NTC):
                dve.wait_ge(y_tr, c + 1)
                v.scalar_tensor_tensor(out=xc[:, c * PPC:(c + 1) * PPC, :],
                                       in0=bank[4 + c][0:PT, :].rearrange("p (n c) -> p n c", c=D),
                                       scalar=tg[:, 1:2], in1=xt[:, c * PPC:(c + 1) * PPC, :],
                                       op0=ALU.mult, op1=ALU.add).then_inc(fin_done, 1)

        @block.tensor
        def _(pe):
            pe.wait_ge(consts, NCONST)
            pe.wait_ge(small_in, 16 * NSMALL)
            for n in range(4):
                pe.transpose(bank[n][:, 0:D], w_raw[:, n, :], ident[:, :]).then_inc(wp_tr, 1)

            def transpose_tokens(c):
                for i in range(PPC):
                    last = pe.transpose(bank[c][:, i * PT:(i + 1) * PT], xc[:, c * PPC + i, :], ident[0:PT, 0:PT])
                last.then_inc(xn_tr, 1)

            pe.wait_ge(ln_done, 1)
            pe.wait_ge(wp_cp, 4)
            pe.wait_ge(wp_lo, 2)
            for c in range(NTC):
                transpose_tokens(c)
            for c in range(NTC):
                pe.wait_ge(xn_cp, c + 1)
                pe.matmul(bank[4 + c][:, 0:TC], wqT[:, :], xnT[:, c * TC:(c + 1) * TC], start=True, stop=True)\
                  .then_inc(q_mm, 1)
            pe.transpose(bank[0][:, 0:I], sh_raw[0:I, 0, :], ident[0:I, 0:I]).then_inc(sh_tr, 1)
            pe.transpose(bank[1][0:I, 0:D], sh_raw[:, 1, 0:I], ident[:, :]).then_inc(sh_tr, 1)
            for a in range(2):
                last = pe.transpose(bank[2][:, a * (E // 2):(a + 1) * (E // 2)], r_raw[:, a, :],
                                    ident[0:E // 2, 0:E // 2])
            last.then_inc(sh_tr, 1)
            pe.wait_ge(gates, 3)
            pe.matmul(bank[3][0:PT, 0:D], bv_rep[:, :], woT[:, :], start=True, stop=True).then_inc(cv_mm, 1)
            pe.wait_ge(q_hi_done, NTC)
            pe.wait_ge(q_lo_done, NTC)
            pe.wait_ge(sh_cp, 3)
            pe.wait_ge(sh_lo, 2)
            pe.wait_ge(pre_done, 1)
            pe.wait_ge(wo_rows, 16 * H)

            def value_product(bt, j, half):
                h, u = bt
                b = num(bt)
                if half == 0:
                    pe.wait_ge(exp_done, b * (2 * KT) + (2 * j + 2))
                    if j % TPC == 0:
                        pe.wait_ge(v_copied, b * NCH + (j // TPC + 1))
                    if j == 0:
                        until(pe, o_copied, b)
                for g in range(3 * half, 3 * half + 3):
                    w = VC if g < 5 else T
                    last = pe.matmul(OB[32 * (g % 4):32 * (g % 4) + 32, (g // 4) * VC:(g // 4) * VC + w],
                                     v_sb[:, u, j, g, :], p_exp[:, j % PR, VC * g:VC * g + w],
                                     start=(j == 0 and g < 4), stop=(j == KT - 1), skip_group_check=True)
                if half == 1:
                    last.then_inc(pv_done, 1)

            def scores(bt, j, f):
                h, u = bt
                b = num(bt)
                if j == 0 and f == 0:
                    pe.wait_ge(kst_here[u], h * (16 * 3 * HG) + 16 * 3 * HG)
                    pe.wait_ge(row_here[u], h * 16 + 16)
                until(pe, exp_done, b * (2 * KT) + (2 * j + f - 1))
                for g in (2 * f, 2 * f + 1):
                    last = pe.matmul(ST[f][0:KP, (g % 2) * GC:(g % 2 + 1) * GC],
                                     k_stk[:, u, g, j * KP:(j + 1) * KP],
                                     q_st[:, u, g, :, :].rearrange("p a t -> p (a t)"), start=True, stop=True)
                last.then_inc(st_done, 1)

            def maxima(step, i):
                u = back(step, 1)[1]
                b = num(back(step, 1))
                m, c = i // NCH, i % NCH
                if i == 0:
                    pe.wait_ge(qblk_made, b + 1)
                    pe.wait_ge(k_hi_done, b * NCH + NCH)
                until(pe, sm_maxed, b * (MT * NCH) + (i - 1))
                rows = q_blk[:, u, :, :].rearrange("p a t -> p (a t)")[:, 128 * m:128 * m + 128]
                pe.matmul(SM[(u + i) % 2][:, 0:CK], rows, kparts[:, u, 0, c * CK:(c + 1) * CK],
                          start=True, stop=True).then_inc(sm_done, 1)

            def body(step):
                for k in range(KT):
                    js, bs, scores_there = tile_at(step, k, 0)
                    jv, bv_, values_there = tile_at(step, k, 1)
                    for f in range(2):
                        if scores_there:
                            scores(bs, js, f)
                        if f == 0 and on(step, 1) and 2 * k < MT * NCH:
                            maxima(step, 2 * k)
                        if values_there:
                            value_product(bv_, jv, f)
                    if on(step, 1) and 2 * k + 1 < MT * NCH:
                        maxima(step, 2 * k + 1)
                    c = k // TPC
                    if on(step, 0):
                        h, u = step
                        b = num(step)
                        if k % TPC == 0:
                            if c == 0:
                                pe.wait_ge(ctx_here[u], h * 16 + 16)
                            until(pe, k_hi_done, b * NCH + c)
                            until(pe, k_lo_done, b * NCH + c)
                            for i in range(TPC):
                                last = pe.transpose(pj(step, "T", c)[:, i * KP:(i + 1) * KP],
                                                    ctx_in[:, u, c * TPC + i, :], ident[0:KP, 0:KP])
                            last.then_inc(t_done, 1)
                        if k % TPC == 2:
                            pe.wait_ge(ct_lo, b * NCH + (c + 1))
                            until(pe, v_copied, (b - 1) * NCH + c)
                            for i, (w, part) in enumerate(((wk_hi, 0), (wk_lo, 0), (wk_hi, 1))):
                                last = pe.matmul(pj(step, "K", c)[:, 0:CK], w[:, :],
                                                 ctT[:, u, part, c * CK:(c + 1) * CK], start=(i == 0), stop=(i == 2))
                            last.then_inc(kp_done, 1)
                    if on(step, 1) and k % TPC == 3:
                        u = back(step, 1)[1]
                        b = num(back(step, 1))
                        if on(step, 0):
                            pe.wait_ge(ct_lo, (b + 1) * NCH + (c + 1))
                        else:
                            pe.wait_ge(k_lo_done, (b + 1) * NCH)
                            pe.wait_ge(v_copied, b * NCH + c)
                        for i in range(TPC):
                            cols = slice((c * TPC + i) * KP, (c * TPC + i + 1) * KP)
                            for n, (part, w) in enumerate(((0, wv_hi), (0, wv_lo), (1, wv_hi))):
                                last = pe.matmul(pj(step, "V", c)[0:KP, i * D:(i + 1) * D], ctT[:, u, part, cols],
                                                 w[:, :], start=(n == 0), stop=(n == 2))
                        last.then_inc(vp_done, 1)
                    if on(step, 0):
                        h, u = step
                        for n, (at, i) in enumerate(PREP_AT[u]):
                            if at == k:
                                pe.wait_ge(w_here[i], h * 32 + 32)
                                until(pe, w_lo_done, h * WPP + i)
                                if n == 0:
                                    until(pe, neg_copied, num(back(step, 1)))
                                if at > DEN_AT and on(step, 3):
                                    pe.wait_ge(rec_done, num(back(step, 3)) * 2 + 2)
                                for a in range(2):
                                    last = pe.transpose(EB[:, a * 128:(a + 1) * 128], w_in[:, i, a, :], ident[:, :])
                                last.then_inc(w_tr, 1)
                    if on(step, 3) and k == DEN_AT:
                        b = num(back(step, 3))
                        if on(step, 0):
                            done = [i for at, i in PREP_AT[step[1]] if at < DEN_AT][-1]
                            pe.wait_ge(w_lo_done, step[0] * WPP + (done + 1))
                        else:
                            pe.wait_ge(neg_copied, min(num(back(step, 1)), B))
                            pe.wait_ge(w_lo_done, EP)
                            pe.wait_ge(x2_done, b // 2)
                        pe.wait_ge(o_copied, b + 1)
                        pe.matmul(EB[:, 0:2 * VC], den_pick[:, :], o_raw[:, :], start=True, stop=True)\
                          .then_inc(den_done, 1)
                    if on(step, 3) and k == OUT_AT and back(step, 3)[1] == 1:
                        h = back(step, 3)[0]
                        if on(step, 0):
                            pe.wait_ge(w_lo_done, step[0] * WPP + (PREP_AT[step[1]][-1][1] + 1))
                        pe.wait_ge(nrm_done, h * 2 + 2)
                        for n in range(6):
                            last = pe.matmul(EB[0:PT, 0:D], o_nrm[:, n, :, :].rearrange("p a t -> p (a t)"),
                                             wo_m[:, n // 3, n % 3, :], start=(n == 0), stop=(n == 5))
                        last.then_inc(op_done, 1)
                    if on(step, 1) and k == NEG_AT:
                        b = num(back(step, 1))
                        if on(step, 0):
                            pe.wait_ge(w_lo_done, step[0] * WPP + (PREP_AT[step[1]][-1][1] + 1))
                        if on(step, 3):
                            pe.wait_ge(rec_done, num(back(step, 3)) * 2 + 2)
                            if back(step, 3)[1] == 1:
                                pe.wait_ge(x2_done, back(step, 3)[0] + 1)
                        pe.wait_ge(neg_made, b + 1)
                        pe.transpose(EB[0:MT, 0:64].bitcast(fp16), neg_max[:, :], ident16[:, :]).then_inc(neg_tr, 1)

            attention(pe, body)

            pe.wait_ge(ln_done, 2)
            for c in range(NTC):
                transpose_tokens(c)
            pe.wait_ge(x2_done, NP)
            for q in range(6):
                n = min(3, NP - 3 * q)
                pe.wait_ge(xf_cp, min(NTC, (3 * q + n - 1) // PPC + 1))
                if q >= 4:
                    pe.wait_ge(lg_biased, q - 3)
                for i in range(n):
                    last = pe.matmul(bank[4 + q % 4][0:PT, i * E:(i + 1) * E],
                                     xnT[:, (3 * q + i) * PT:(3 * q + i + 1) * PT], rT[:, :], start=True, stop=True)
                last.then_inc(lg_mm, 1)
            pe.wait_ge(parts_done, 1)
            for n in range(NP):
                if n >= 4:
                    pe.wait_ge(cb_cp, n - 3)
                out_b = bank[4 + n % 4][0:PW, 0:EG * PT // 2].bitcast(bf16)
                for g in range(EG):
                    last = pe.transpose(out_b[:, g * PT:(g + 1) * PT], parts[:, n, g, :], identb[0:PT, 0:PT])
                last.then_inc(cb_tr, 1)
            pe.wait_ge(cb_cp, NP)
            pe.wait_ge(xl_cp, NTC)

            hilo = ((0, 0), (1, 0), (0, 1))
            xparts = (q_hi, q_lo)
            hparts = (h_hi, h_lo)
            for t in range(NTC):
                if t >= 2:
                    pe.wait_ge(s_done, t - 1)
                for i, (a, b) in enumerate(hilo):
                    last = pe.matmul(ZB[t % 2][0:I, 0:TC], sg[:, a, :], xparts[b][:, t * TC:(t + 1) * TC],
                                     start=(i == 0), stop=(i == 2))
                last.then_inc(z_done, 1)

            def down(n, t, q, shared=False, end=False):
                pe.wait_ge(hl_done, n * NTC + (NTC + t + 1))
                for i, (a, b) in enumerate(hilo):
                    rows = slice(0, I if shared else 128)
                    w = sd[:, a, :] if shared else w_ring[:, q, 2 + a, :]
                    last = pe.matmul(YB[t][:, 0:TC], w, hparts[b][rows, t, :], start=(shared and i == 0),
                                     stop=(end and i == 2), skip_group_check=True)
                last.then_inc(dn_done, 1)

            def pairs(i, g, first=False):
                for q in range(WR):
                    n = i * WR + q
                    for t in range(NTC):
                        m = n * NTC + (NTC + t)
                        down(n - 1, t, (q - 1) % WR, shared=first and q == 0)
                        if t == 0:
                            pe.wait_ge(ring_here[q], i * 16 + 16)
                        pe.wait_ge(s_done, m - 1)
                        for j, (a, b) in enumerate(hilo):
                            last = pe.matmul(ZB[t % 2][:, 0:TC], w_ring[:, q, a, :], xparts[b][:, t * TC:(t + 1) * TC],
                                             start=(j == 0), stop=(j == 2))
                        last.then_inc(z_done, 1)
                        if not (first and q == 0 and t < 2):
                            pe.wait_ge(h_done, m - (NTC + 1))
                        at = (n - g * GP) * 128
                        pe.matmul(CB[t % 2][:, 0:TC], expand[0:PW, :, :].rearrange("p e i -> p (e i)")[:, bass.ds(at, 128)],
                                  combT[0:PW, g, t * TC:(t + 1) * TC], start=True, stop=True).then_inc(c_done, 1)

            pairs(0, 0, True)
            for g in range(EG):
                with pe.Fori(g * GP // WR + (1 if g == 0 else 0), (g + 1) * GP // WR) as i:
                    pairs(i, g)
            for t in range(NTC):
                down(EP - 1, t, WR - 1, end=True)
            for c in range(NTC):
                pe.wait_ge(y_cp, c + 1)
                for i in range(PPC):
                    last = pe.transpose(bank[4 + c][0:PT, i * D:(i + 1) * D],
                                        xnT[:, (c * PPC + i) * PT:(c * PPC + i + 1) * PT], ident[:, :])
                last.then_inc(y_tr, 1)


_INS = ['x', 'ctx_1024', 'g_xattn', 'g_ffn', 'L0_xattn_Wq', 'L0_xattn_bq', 'L0_xattn_Wk', 'L0_xattn_bk',
        'L0_xattn_Wv', 'L0_xattn_bv', 'L0_xattn_Wo', 'L0_xattn_bo', 'L0_ffn_router_w', 'L0_ffn_expert_bias',
        'L0_ffn_w_gate', 'L0_ffn_w_down', 'L0_ffn_w_gate_shared', 'L0_ffn_w_down_shared']
_OUTS = [((32, 56, 128), 'float32')]


def kernel(**inputs):
    import numpy as _np
    import concourse.bacc as _bacc
    from concourse import mybir as _mybir
    from concourse.bass_utils import run_bass_kernel_spmd as _run

    nc = _bacc.Bacc("TRN2", target_bir_lowering=False, num_devices=1)
    arrays, args = {}, []
    for name in _INS:
        a = _np.ascontiguousarray(inputs[name])
        arrays[f"in_{name}_dram"] = a
        args.append(nc.dram_tensor(f"in_{name}_dram", a.shape, _mybir.dt.from_np(a.dtype), kind="ExternalInput").ap())
    for i, (shape, dtype) in enumerate(_OUTS):
        dt = _mybir.dt.from_np(_np.dtype(dtype))
        args.append(nc.dram_tensor(f"out_{i}_dram", shape, dt, kind="ExternalOutput").ap())
    flamingo_gated_block(nc, *args)
    r = _run(nc, [arrays], core_ids=[0])
    got = tuple(r.results[0][f"out_{i}_dram"] for i in range(len(_OUTS)))
    return got[0]
```

```python
import concourse.bass as bass
from concourse import mybir
from contextlib import ExitStack


def flamingo_gated_block(nc, x, ctx, g_xattn, g_ffn, Wq, bq, Wk, bk, Wv, bv, Wo, bo,
                         router_w, expert_bias, w_gate, w_down, w_gate_shared, w_down_shared, out):
    fp32 = mybir.dt.float32
    fp16 = mybir.dt.float16
    bf16 = mybir.dt.bfloat16
    ALU = mybir.AluOpType
    ACT = mybir.ActivationFunctionType
    AX = mybir.AxisListType

    B, T, D = x.shape
    C = ctx.shape[1]
    H = 16
    d = D // H
    E, I, _ = w_gate.shape
    TOP_K = 8
    ROUTED_SCALE = 2.5
    EPS_LN = 1e-5
    EPS_TOPK = 1e-9
    QSCALE = float(d) ** -0.5

    N = B * T
    PT = 2 * T
    NP = B // 2
    HT = H * T
    KT = 12
    KP = C // KT
    NCH = 3
    CK = C // NCH
    TPC = KT // NCH
    MT = HT // 128
    HG = 4
    GC = HT // HG
    VG = 8
    VC = 3 * T
    OC = 4 * T
    PR = 3
    NTC = 4
    TC = N // NTC
    PPC = NP // NTC
    EG = 4
    GE = E // EG
    EP = E // 2
    GP = GE // 2
    WPP = EP // (B // 2)
    WR = 4
    LAG = 2
    PREP_AT = {0: [(1, 0), (3, 1), (7, 2)], 1: [(1, 3), (7, 4)]}
    DEN_AT, OUT_AT, NEG_AT = 5, 9, KT - 1

    stk = ExitStack()
    with stk:
        def sb(name, shape, dt=fp32):
            return stk.enter_context(nc.sbuf_tensor(name, shape, dt))

        def sem(name):
            return stk.enter_context(nc.semaphore(name))

        ident = sb("ident", [128, 128])
        ident16 = sb("ident16", [128, 128], fp16)
        identb = sb("identb", [128, 128], bf16)
        head_mask = sb("head_mask", [128, H], fp16)
        stack_mask = sb("stack_mask", [96, HG], fp16)
        den_pick = sb("den_pick", [128, 128])
        expand = sb("expand", [128, GE, I], bf16)
        ones_d = sb("ones_d", [D, PT])
        w_raw = sb("w_raw", [128, 4, D])
        wqT = sb("wqT", [D, D])
        woT = sb("woT", [D, D])
        wk_hi = sb("wk_hi", [D, D], fp16)
        wk_lo = sb("wk_lo", [D, D], fp16)
        wv_hi = sb("wv_hi", [D, D], fp16)
        wv_lo = sb("wv_lo", [D, D], fp16)
        wo_m = sb("wo_m", [128, 4, D])
        bqc = sb("bqc", [D, 1])
        bqs = sb("bqs", [D, 1])
        bkc = sb("bkc", [D, 1])
        bvc = sb("bvc", [D, 1])
        bv_rep = sb("bv_rep", [D, PT])
        bo_b = sb("bo_b", [PT, D])
        eb_b = sb("eb_b", [PT, E])
        g_raw = sb("g_raw", [PT, 2])
        tg = sb("tg", [PT, 2])
        xt = sb("xt", [PT, NP, D])
        xc = sb("xc", [PT, NP, D])
        stat = sb("stat", [PT, 5, NP])
        xnT = sb("xnT", [D, N])
        q_hi = sb("q_hi", [D, N], fp16)
        q_lo = sb("q_lo", [D, N], fp16)
        q_stk = sb("q_stk", [128, HG, N], fp16)
        ctx_in = sb("ctx_in", [KP, 2, KT, D])
        ctT = sb("ctT", [D, 2, 2, C], fp16)
        kparts = sb("kparts", [D, 2, 2, C], fp16)
        k_stk = sb("k_stk", [128, 2, HG, C], fp16)
        v_sb = sb("v_sb", [KP, 2, KT, VG, 32])
        q_blk = sb("q_blk", [D, 2, H, T], fp16)
        q_st = sb("q_st", [128, 2, HG, HG, T], fp16)
        part_max = sb("part_max", [128, MT, NCH])
        neg_max = sb("neg_max", [128, MT], fp16)
        neg_row = sb("neg_row", [MT, 128], fp16)
        p_exp = sb("p_exp", [128, PR, HT])
        o_raw = sb("o_raw", [128, OC])
        o_rec = sb("o_rec", [128, OC])
        o_nrm = sb("o_nrm", [128, 4, 2, T])
        w_in = sb("w_in", [128, WPP, 2, 128])
        w_out = sb("w_out", [128, WPP, 4, 128], fp16)
        w_ring = sb("w_ring", [128, WR, 4, 128], fp16)
        sh_raw = sb("sh_raw", [128, 2, D])
        sg = sb("sg", [128, 2, I], fp16)
        sd = sb("sd", [I, 2, D], fp16)
        r_raw = sb("r_raw", [E // 2, 2, D])
        rT = sb("rT", [D, E])
        top = sb("top", [PT, NP, TOP_K])
        wsum = sb("wsum", [PT, 3, NP])
        w_scratch = nc.dram_tensor("w_scratch", [EP, 128, 4, 128], fp16, kind="Internal").ap()

        def flat(ap, pattern, dt=None):
            a = ap.rearrange(pattern)
            return a.bitcast(dt) if dt is not None else a

        k_words = flat(kparts[:, :, :, :], "p a b c -> p (a b c)", fp32)
        sq = flat(p_exp[0:PT, :, :], "p a b -> p (a b)")[:, 0:NP * D].rearrange("p (n c) -> p n c", c=D)
        q_tmp = flat(p_exp[:, :, :], "p a b -> p (a b)")[:, 0:TC]
        s_act = k_words[:, 0:2 * TC].rearrange("p (a t) -> p a t", a=2)
        prob = flat(p_exp[0:PT, :, :], "p a b -> p (a b)")[:, 0:NP * E].rearrange("p (n e) -> p n e", e=E)
        c_words = flat(ctx_in[:, :, :, :], "p a b c -> p (a b c)")
        rep = c_words[0:PT, 0:NP * E].rearrange("p (n e) -> p n e", e=E)
        comb = flat(v_sb[0:PT, :, :, :, :], "p a b c e -> p (a b c e)")[:, 0:NP * E].rearrange("p (n e) -> p n e", e=E)
        PW = 3 * GE
        parts = flat(k_stk[0:PT, :, :, :], "p a b c -> p (a b c)", bf16)[:, 0:NP * EG * PW]\
            .rearrange("p (n g w) -> p n g w", g=EG, w=PW)
        combT = q_stk[:, :, :].bitcast(bf16)
        h_words = flat(k_stk[:, :, :, :], "p a b c -> p (a b c)", fp32)
        h_f = h_words[:, 0:NTC * TC].rearrange("p (a t) -> p a t", a=NTC)
        t_words = flat(ctT[:, :, :, :], "p a b c -> p (a b c)")
        h_hi = t_words[:, 0:NTC * TC].rearrange("p (a t) -> p a t", a=NTC)
        h_lo = t_words[:, NTC * TC:2 * NTC * TC].rearrange("p (a t) -> p a t", a=NTC)

        bank = [stk.enter_context(nc.psum_tensor(f"bank{i}", [128, 512], fp32)) for i in range(8)]
        ST = [bank[0], bank[1]]
        SM = [bank[2], bank[3]]
        OB = bank[4]
        PJ = [bank[5], bank[6]]
        EB = bank[7]
        SH = bank[4]
        YB = [bank[0], bank[1], bank[2], bank[3]]
        ZB = [bank[4], bank[5]]
        CB = [bank[6], bank[7]]

        names = """consts weights_in small_in late_in x_in wp_tr wp_cp wp_lo ln_sub ln_sq ln_var ln_root ln_done xn_tr xn_cp bqs_made gates_made bv_made
            q_mm q_hi_done q_lo_done q_rows wo_rows cv_mm pre_done sh_tr sh_cp sh_lo o_cleared
            t_done ct_hi ct_lo kp_done k_hi_done k_lo_done vp_done v_copied qblk_made qst_made
            sm_done sm_maxed neg_made neg_tr neg_copied st_done exp_done pv_done o_copied den_done rec_done
            nrm_done op_done x2_done w_tr w_hi_done w_lo_done
            xf_cp xh_cp xl_cp lg_mm lg_biased prob_done top_done comb_done part_cast part_rest parts_done cb_tr cb_cp
            z_done c_done s_done h_done hh_done hl_done dn_done y_cp y_tr fin_done stored dve_chain""".split()
        S = {name: sem(name) for name in names}
        (consts, weights_in, small_in, late_in, x_in, wp_tr, wp_cp, wp_lo, ln_sub, ln_sq, ln_var, ln_root, ln_done, xn_tr, xn_cp, bqs_made, gates_made, bv_made,
         q_mm, q_hi_done, q_lo_done, q_rows, wo_rows, cv_mm, pre_done, sh_tr, sh_cp, sh_lo, o_cleared,
         t_done, ct_hi, ct_lo, kp_done, k_hi_done, k_lo_done, vp_done, v_copied, qblk_made, qst_made,
         sm_done, sm_maxed, neg_made, neg_tr, neg_copied, st_done, exp_done, pv_done, o_copied, den_done, rec_done,
         nrm_done, op_done, x2_done, w_tr, w_hi_done, w_lo_done,
         xf_cp, xh_cp, xl_cp, lg_mm, lg_biased, prob_done, top_done, comb_done, part_cast, part_rest, parts_done, cb_tr, cb_cp,
         z_done, c_done, s_done, h_done, hh_done, hl_done, dn_done, y_cp, y_tr, fin_done, stored, dve_chain) = \
            [S[name] for name in names]
        ctx_here = [sem(f"ctx_here{i}") for i in range(2)]
        kst_here = [sem(f"kst_here{i}") for i in range(2)]
        row_here = [sem(f"row_here{i}") for i in range(2)]
        w_here = [sem(f"w_here{i}") for i in range(WPP)]
        w_stored = [sem(f"w_stored{i}") for i in range(WPP)]
        ring_here = [sem(f"ring_here{i}") for i in range(WR)]
        IDENT, MASKS, V_ONES, K_ONES, NCONST = 2, 12, 13, 14, 18
        NSMALL = 7

        def back(hu, n):
            v = hu[1] - n
            return (hu[0] + v // 2, v % 2)

        def num(hu):
            return hu[0] * 2 + hu[1]

        def on(step, n):
            return not isinstance(step[0], int) or 0 <= num(step) - n < B

        def until(eng, s, value):
            if not isinstance(value, int) or value > 0:
                eng.wait_ge(s, value)

        def attention(eng, body, loop_to=B, before={}):
            for s in range(4):
                if s in before:
                    before[s]()
                body((s // 2, s % 2))
            with eng.Fori(2, loop_to // 2) as h:
                body((h, 0))
                body((h, 1))
            for s in range(loop_to, B + 3):
                body((s // 2, s % 2))

        def tile_at(step, k, late):
            j = k - LAG - late
            return (j, back(step, 2), on(step, 2)) if j >= 0 else (j + KT, back(step, 3), on(step, 3))

        def pj(step, kind, c):
            return PJ[(step[1] + 3 * c + "TKV".index(kind)) % 2]

        def row(ap):
            return ap.rearrange("(a n) -> a n", a=1)

        x_pairs = x.rearrange("(n b) t c -> (b t) n c", b=2)
        out_pairs = out.rearrange("(n b) t c -> (b t) n c", b=2)
        gate_pairs = w_gate.rearrange("(n e) i h -> n (e i) h", e=2)
        down_pairs = w_down.rearrange("(n e) h i -> n h e i", e=2)

        block = stk.enter_context(nc.Block())

        @block.sync
        def _(sp):
            for b in range(2):
                sp.dma_start(xt[b * T:(b + 1) * T, :, :], x.rearrange("(n b) t c -> b t n c", b=2)[b]).then_inc(x_in, 16)
            for n, w in enumerate((Wq, Wk, Wv, Wo)):
                sp.dma_start(w_raw[:, n, :], w).then_inc(weights_in, 16)
            for dst, src in ((bqc, bq), (bkc, bk), (bvc, bv)):
                sp.dma_start(dst[:, :], src.rearrange("(p a) -> p a", a=1)).then_inc(small_in, 16)
            sp.dma_start(ctx_in[:, 0, :, :], ctx[0].rearrange("(p j) c -> p j c", j=KT)).then_inc(ctx_here[0], 16)
            sp.dma_start(bo_b[:, :], row(bo).to_broadcast([PT, D])).then_inc(small_in, 16)
            sp.dma_start(eb_b[:, :], row(expert_bias).to_broadcast([PT, E])).then_inc(small_in, 16)
            for n, g in enumerate((g_xattn, g_ffn)):
                sp.dma_start(g_raw[:, n:n + 1], row(g).to_broadcast([PT, 1])).then_inc(small_in, 16)
            sp.dma_start(ctx_in[:, 1, :, :], ctx[1].rearrange("(p j) c -> p j c", j=KT)).then_inc(ctx_here[1], 16)
            sp.dma_start(sh_raw[0:I, 0, :], w_gate_shared).then_inc(late_in, 16)
            sp.dma_start(sh_raw[:, 1, 0:I], w_down_shared).then_inc(late_in, 16)
            sp.dma_start(r_raw[:, :, :], router_w.rearrange("(a p) h -> p a h", a=2)).then_inc(late_in, 16)
            sp.wait_ge(wp_cp, 4)
            sp.wait_ge(o_cleared, 1)
            for h in range(H):
                g, c = (h // 3, h % 3) if h < 12 else (h - 12, 3)
                p0 = 32 * g + (d * c if c < 3 else 0)
                sp.dma_start(wo_m[p0:p0 + d, c, :], woT[d * h:d * h + d, :]).then_inc(wo_rows, 16)
            sp.wait_ge(q_hi_done, NTC)
            sp.wait_ge(q_lo_done, NTC)
            for g in range(HG):
                for r, part in enumerate((q_hi, q_lo, q_hi)):
                    sp.dma_start(q_stk[32 * r:32 * r + 32, g, :], part[32 * g:32 * g + 32, :]).then_inc(q_rows, 16)

            def body(step):
                if on(step, 1):
                    h, u = back(step, 1)
                    b = num((h, u))
                    read, made = (b - 1) * (2 * KT), b * NCH + NCH
                    if not isinstance(h, int):
                        read, made = sp.to_reg(read), sp.to_reg(made)
                    until(sp, st_done, read)
                    sp.wait_ge(k_lo_done, made)
                    for g in range(HG):
                        for r, part in enumerate((0, 0, 1)):
                            sp.dma_start(k_stk[32 * r:32 * r + 32, u, g, :], kparts[32 * g:32 * g + 32, u, part, :])\
                              .then_inc(kst_here[u], 16)
                if on(step, -1) and not (isinstance(step[0], int) and num(step) < 1):
                    h, u = back(step, -1)
                    b = num((h, u))
                    sp.wait_ge(t_done, (b - 1) * NCH)
                    sp.dma_start(ctx_in[:, u, :, :], ctx[bass.ds(b, 1)].rearrange("a (p j) c -> p (a j) c", j=KT))\
                      .then_inc(ctx_here[u], 16)
                if on(step, 1):
                    u = back(step, 1)[1]
                    b = num(back(step, 1))
                    sp.wait_ge(qst_made, b + 1)
                    sp.wait_ge(neg_copied, b + 1)
                    sp.dma_start(q_st[96:97, u, :, :, :].rearrange("p a b c -> p (a b c)"), neg_row[:, :])\
                      .then_inc(row_here[u], 16)

            attention(sp, body, B - 2)

            for i in range(WPP):
                sp.wait_ge(w_stored[i], 16 * (B // 2))
            for n in range(WR):
                sp.dma_start(w_ring[:, n, :, :], w_scratch[n]).then_inc(ring_here[n], 16)
            with sp.Fori(1, EP // WR) as i:
                for q in range(WR):
                    sp.wait_ge(dn_done, i * (WR * NTC) + (q - WR + 2) * NTC)
                    sp.dma_start(w_ring[:, q, :, :], w_scratch[bass.ds(i * WR + q, 1)].rearrange("a p b c -> p (a b) c"))\
                      .then_inc(ring_here[q], 16)
            for c in range(NTC):
                sp.wait_ge(fin_done, c + 1)
                for b in range(2):
                    sp.dma_start(out.rearrange("(n b) t c -> b t n c", b=2)[b, :, c * PPC:(c + 1) * PPC, :],
                                 xc[b * T:(b + 1) * T, c * PPC:(c + 1) * PPC, :]).then_inc(stored, 16)
            sp.wait_ge(stored, 16 * 2 * NTC)

        @block.gpsimd
        def _(pool):
            made = [0]

            def const(ins):
                made[0] += 1
                ins.then_inc(consts, 1)
                pool.wait_ge(consts, made[0])

            const(pool.memset(ident[:, :], 0.0))
            const(pool.affine_select(out=ident[:, :], in_=ident[:, :], compare_op=ALU.not_equal, fill=1.0,
                                     base=0, pattern=[[-1, 128]], channel_multiplier=1))
            assert made[0] == IDENT
            const(pool.memset(head_mask[:, :], 1.0))
            const(pool.affine_select(out=head_mask[:, :], in_=head_mask[:, :], compare_op=ALU.is_ge, fill=0.0,
                                     base=0, pattern=[[-d, H]], channel_multiplier=1))
            const(pool.affine_select(out=head_mask[:, :], in_=head_mask[:, :], compare_op=ALU.is_ge, fill=0.0,
                                     base=d - 1, pattern=[[d, H]], channel_multiplier=-1))
            const(pool.tensor_copy(ident16[:, :], ident[:, :]))
            const(pool.tensor_copy(identb[:, :], ident[:, :]))
            for r in range(3):
                const(pool.tensor_copy(stack_mask[32 * r:32 * r + 32, :], head_mask[32 * r:32 * r + 32, 4 * r:4 * r + 4]))
            const(pool.memset(den_pick[:, :], 0.0))
            dp = den_pick[:, :].rearrange("p (a b) -> p a b", b=32)
            const(pool.affine_select(out=dp, in_=dp, compare_op=ALU.not_equal, fill=1.0,
                                     base=3 * d, pattern=[[32, 4], [0, 32]], channel_multiplier=-1))
            assert made[0] == MASKS

            def load_pair(step):
                for _, i in PREP_AT[step[1]]:
                    h = step[0]
                    until(pool, w_tr, h * WPP + (i + 1 - WPP))
                    pool.dma_start(w_in[:, i, 0, :], gate_pairs[bass.ds(h * WPP + i, 1)].rearrange("a p c -> p (a c)"))\
                        .then_inc(w_here[i], 16)
                    pool.dma_start(w_in[:, i, 1, :].rearrange("p (e c) -> p e c", e=2),
                                   down_pairs[bass.ds(h * WPP + i, 1)].rearrange("a h e c -> h (a e) c"))\
                        .then_inc(w_here[i], 16)

            def store_pair(step):
                for _, i in PREP_AT[step[1]]:
                    h = step[0]
                    pool.wait_ge(w_hi_done, h * WPP + (i + 1))
                    pool.wait_ge(w_lo_done, h * WPP + (i + 1))
                    pool.dma_start(w_scratch[bass.ds(h * WPP + i, 1)].rearrange("a p b c -> p (a b) c"), w_out[:, i, :, :])\
                        .then_inc(w_stored[i], 16)

            def ones():
                const(pool.memset(v_sb[:, :, :, :, :], 1.0))
                assert made[0] == V_ONES
                const(pool.memset(k_stk[96:97, :, :, :], 1.0))
                assert made[0] == K_ONES
                pool.wait_ge(q_rows, 16 * 3 * HG)

            def spread():
                const(pool.memset(expand[:, :, :], 0.0))
                for r in range(3):
                    const(pool.affine_select(out=expand[:, :, :], in_=expand[:, :, :], compare_op=ALU.not_equal,
                                             fill=1.0, base=GE * r, pattern=[[1, GE], [0, I]], channel_multiplier=-1))
                assert made[0] == NCONST

            load_pair((0, 0))
            pool.wait_ge(q_hi_done, NTC)

            def body(step):
                if on(step, 0):
                    h, u = step
                    b = num(step)
                    until(pool, sm_done, (b - 1) * (MT * NCH))
                    pool.tensor_tensor(q_blk[:, u, :, :],
                                       q_hi[:, bass.ds(b * T, T)].unsqueeze(1).to_broadcast([D, H, T]),
                                       head_mask[:, :].unsqueeze(2).to_broadcast([D, H, T]), ALU.mult)\
                        .then_inc(qblk_made, 1)
                if on(step, 1):
                    store_pair(back(step, 1))
                if on(step, -1):
                    load_pair(back(step, -1))
                if on(step, 1):
                    h, u = back(step, 1)
                    b = num((h, u))
                    until(pool, st_done, (b - 1) * (2 * KT))
                    for g in range(HG):
                        last = pool.tensor_tensor(q_st[0:96, u, g, :, :],
                                                  q_stk[0:96, g, bass.ds(b * T, T)].unsqueeze(1).to_broadcast([96, HG, T]),
                                                  stack_mask[:, :].unsqueeze(2).to_broadcast([96, HG, T]), ALU.mult)
                    last.then_inc(qst_made, 1)

            attention(pool, body, B - 2, {1: ones, 2: spread})

        @block.scalar
        def _(act):
            for n, w in enumerate((wqT, wk_hi, wv_hi, woT)):
                act.wait_ge(wp_tr, n + 1)
                act.activation(w[:, :], bank[n][:, 0:D], ACT.Copy).then_inc(wp_cp, 1)
            act.wait_ge(small_in, 16 * NSMALL)
            act.activation(bqs[:, :], bqc[:, :], ACT.Copy, scale=QSCALE).then_inc(bqs_made, 1)

            def norm_act(n):
                act.wait_ge(ln_sub, n)
                act.activation(sq, xc[:, :, :], ACT.Square).then_inc(ln_sq, 1)
                act.wait_ge(ln_var, n)
                act.activation(stat[:, 3, :], stat[:, 2, :], ACT.Sqrt).then_inc(ln_root, 1)

            norm_act(1)
            for c in range(NTC):
                act.wait_ge(xn_tr, c + 1)
                act.activation(xnT[:, c * TC:(c + 1) * TC], bank[c][:, 0:TC], ACT.Copy).then_inc(xn_cp, 1)
            act.wait_ge(bqs_made, 1)
            for c in range(NTC):
                act.wait_ge(q_mm, c + 1)
                act.activation(q_hi[:, c * TC:(c + 1) * TC], bank[c][:, 0:TC], ACT.Identity,
                               bias=bqs[:, 0:1], scale=QSCALE).then_inc(q_hi_done, 1)

            def gates_and_shared():
                act.activation(tg[:, :], g_raw[:, :], ACT.Tanh).then_inc(gates_made, 1)
                act.wait_ge(cv_mm, 1)
                act.wait_ge(sh_tr, 3)
                act.activation(sg[:, 0, :], SH[:, 0:I], ACT.Copy).then_inc(sh_cp, 1)
                act.activation(sd[:, 0, :], SH[0:I, I:I + D], ACT.Copy).then_inc(sh_cp, 1)
                act.activation(rT[:, :], SH[:, I + D:I + D + E], ACT.Copy).then_inc(sh_cp, 1)
                act.wait_ge(consts, V_ONES)

            def body(step):
                for k in range(KT):
                    j, bt, there = tile_at(step, k, 0)
                    for f in range(2):
                        if there:
                            b = num(bt)
                            act.wait_ge(st_done, b * (2 * KT) + (2 * j + f + 1))
                            if f == 0:
                                until(act, pv_done, b * KT + (j - PR + 1))
                            act.activation(p_exp[0:KP, j % PR, f * 448:(f + 1) * 448], ST[f][0:KP, 0:448],
                                           ACT.Exp).then_inc(exp_done, 1)
                        if f == 0:
                            evacuate(step, k - 1)

            def values(bt, bank_v, c):
                u = bt[1]
                b = num(bt)
                act.wait_ge(vp_done, b * NCH + (c + 1))
                if c == 0:
                    until(act, pv_done, (b - 1) * KT)
                src = bank_v[0:KP, :].rearrange("p (j n) -> p j n", n=D)
                act.activation(v_sb[:, u, c * TPC:(c + 1) * TPC, 0:4, 0:3 * d],
                               src[:, :, 0:12 * d].rearrange("p j (g n) -> p j g n", g=4), ACT.Copy)
                act.activation(v_sb[:, u, c * TPC:(c + 1) * TPC, 4:8, 0:d],
                               src[:, :, 12 * d:16 * d].rearrange("p j (g n) -> p j g n", g=4), ACT.Copy)\
                   .then_inc(v_copied, 1)

            def evacuate(step, k):
                if k < 0 and on(step, 2):
                    values(back(step, 2), pj(back(step, 1), "V", NCH - 1), NCH - 1)
                if k % TPC == 3 and k > 0 and on(step, 1):
                    values(back(step, 1), pj(step, "V", k // TPC), k // TPC)
                if k < 0 and on(step, 2):
                    b = num(back(step, 2))
                    act.wait_ge(neg_tr, b + 1)
                    if not (isinstance(b, int) and b == 0):
                        hp, up = back(step, 3)
                        act.wait_ge(row_here[up], hp * 16 + 16)
                    act.activation(neg_row[:, :], EB[0:MT, 0:64].bitcast(fp16), ACT.Copy).then_inc(neg_copied, 1)
                if k >= 0 and on(step, 0):
                    h, u = step
                    b = num(step)
                    c = k // TPC
                    if k % TPC == 0:
                        act.wait_ge(t_done, b * NCH + (c + 1))
                        act.activation(ctT[:, u, 0, c * CK:(c + 1) * CK], pj(step, "T", c)[:, 0:CK],
                                       ACT.Copy).then_inc(ct_hi, 1)
                    if k % TPC == 2:
                        act.wait_ge(kp_done, b * NCH + (c + 1))
                        if c == 0:
                            until(act, sm_done, (b - 1) * (MT * NCH))
                            if not isinstance(h, int) or h > 0:
                                act.wait_ge(kst_here[u], h * (16 * 3 * HG))
                        act.activation(kparts[:, u, 0, c * CK:(c + 1) * CK], pj(step, "K", c)[:, 0:CK],
                                       ACT.Identity, bias=bkc[:, 0:1]).then_inc(k_hi_done, 1)
                    for at, i in PREP_AT[u]:
                        if at == k:
                            act.wait_ge(w_tr, h * WPP + (i + 1))
                            if not isinstance(h, int) or h > 0:
                                act.wait_ge(w_stored[i], h * 16)
                            act.activation(w_out[:, i, 0:4:2, :],
                                           EB[:, 0:256].rearrange("p (a b) -> p a b", a=2),
                                           ACT.Copy).then_inc(w_hi_done, 1)

            attention(act, body, B, {1: gates_and_shared})

            norm_act(2)
            for c in range(NTC):
                act.wait_ge(xn_tr, NTC + c + 1)
                act.activation(q_hi[:, c * TC:(c + 1) * TC], bank[c][:, 0:TC], ACT.Copy).then_inc(xh_cp, 1)
            act.wait_ge(lg_biased, 6)
            act.activation(prob, prob, ACT.Sigmoid).then_inc(prob_done, 1)
            for r in range(2):
                act.wait_ge(comb_done if r == 0 else part_rest, 1)
                act.activation(parts[:, :, :, r * GE:(r + 1) * GE], comb.rearrange("p n (g e) -> p n g e", g=EG),
                               ACT.Copy).then_inc(part_cast, 1)
            for n in range(NP):
                act.wait_ge(cb_tr, n + 1)
                act.activation(combT[0:PW, :, n * PT:(n + 1) * PT],
                               bank[4 + n % 4][0:PW, 0:EG * PT // 2].bitcast(bf16).rearrange("p (g t) -> p g t", g=EG),
                               ACT.Copy).then_inc(cb_cp, 1)
            for t in range(NTC):
                act.wait_ge(z_done, t + 1)
                act.activation(h_f[0:I, t, :], ZB[t % 2][0:I, 0:TC], ACT.Silu).then_inc(s_done, 1)
                act.wait_ge(s_done, t + 1)
                act.activation(h_hi[0:I, t, :], h_f[0:I, t, :], ACT.Copy).then_inc(hh_done, 1)

            def silu(n, t, first=False):
                m = n * NTC + (NTC + t)
                act.wait_ge(z_done, m + 1)
                if not (first and t < 2):
                    act.wait_ge(h_done, m - (NTC + 1))
                act.activation(s_act[:, t % 2, :], ZB[t % 2][:, 0:TC], ACT.Silu).then_inc(s_done, 1)

            def hi_part(n, t):
                act.wait_ge(h_done, n * NTC + (t + 1))
                act.activation(h_hi[:, t, :], h_f[:, t, :], ACT.Copy).then_inc(hh_done, 1)

            def pairs(base, first=False):
                for q in range(WR):
                    for t in range(NTC):
                        f = first and q == 0
                        silu(base + q, t, f)
                        if t:
                            hi_part(base + q, t - 1)
                        elif not f:
                            hi_part(base + (q - 1), NTC - 1)

            pairs(0, True)
            with act.Fori(1, EP // WR) as i:
                pairs(i * WR)
            hi_part(EP - 1, NTC - 1)
            for c in range(NTC):
                act.wait_ge(dn_done, EP * NTC + NTC)
                act.activation(xnT[:, c * TC:(c + 1) * TC], YB[c][:, 0:TC], ACT.Copy).then_inc(y_cp, 1)

        @block.vector
        def _(dve):
            v = nc.vector
            chained = [0]

            def link(ins):
                chained[0] += 1
                ins.then_inc(dve_chain, 1)
                dve.wait_ge(dve_chain, chained[0])

            v.memset(wo_m[:, :, :], 0.0).then_inc(o_cleared, 1)
            v.memset(ones_d[:, :], 1.0).then_inc(o_cleared, 1)

            def norm(n):
                link(v.reduce_sum(stat[:, 0, :], xt[:, :, :], axis=AX.X))
                link(v.tensor_scalar(stat[:, 1, :], stat[:, 0, :], -1.0 / D, None, ALU.mult))
                v.tensor_tensor(xc[:, :, :], xt[:, :, :], stat[:, 1, :].unsqueeze(2).to_broadcast([PT, NP, D]),
                                ALU.add).then_inc(ln_sub, 1)
                dve.wait_ge(ln_sq, n)
                link(v.reduce_sum(stat[:, 0, :], sq, axis=AX.X))
                v.tensor_scalar(stat[:, 2, :], stat[:, 0, :], 1.0 / D, EPS_LN, ALU.mult, ALU.add).then_inc(ln_var, 1)
                dve.wait_ge(ln_root, n)
                link(v.reciprocal(stat[:, 4, :], stat[:, 3, :]))
                v.tensor_tensor(xc[:, :, :], xc[:, :, :], stat[:, 4, :].unsqueeze(2).to_broadcast([PT, NP, D]),
                                ALU.mult).then_inc(ln_done, 1)

            for n, (lo, hi) in enumerate(((wk_lo, wk_hi), (wv_lo, wv_hi))):
                dve.wait_ge(wp_cp, n + 2)
                v.tensor_tensor(lo[:, :], bank[n + 1][:, 0:D], hi[:, :], ALU.subtract).then_inc(wp_lo, 1)
            dve.wait_ge(x_in, 32)
            norm(1)
            dve.wait_ge(small_in, 16 * NSMALL)
            dve.wait_ge(bqs_made, 1)
            for c in range(NTC):
                dve.wait_ge(q_hi_done, c + 1)
                if c:
                    dve.wait_ge(q_lo_done, c)
                link(v.tensor_scalar(q_tmp, bank[c][:, 0:TC], QSCALE, bqs[:, 0:1], ALU.mult, ALU.add))
                v.tensor_tensor(q_lo[:, c * TC:(c + 1) * TC], q_tmp, q_hi[:, c * TC:(c + 1) * TC],
                                ALU.subtract).then_inc(q_lo_done, 1)
            dve.wait_ge(o_cleared, 2)
            v.tensor_scalar(bv_rep[:, :], ones_d[:, :], bvc[:, 0:1], None, ALU.mult).then_inc(bv_made, 1)

            def constant_term():
                dve.wait_ge(cv_mm, 1)
                dve.wait_ge(sh_cp, 3)
                link(v.tensor_tensor(bo_b[:, :], SH[0:PT, I + D + E:I + 2 * D + E], bo_b[:, :], ALU.add))
                dve.wait_ge(gates_made, 1)
                link(v.tensor_scalar(bo_b[:, :], bo_b[:, :], tg[:, 0:1], None, ALU.mult))
                v.tensor_tensor(xt[:, :, :], xt[:, :, :], bo_b[:, :].unsqueeze(1).to_broadcast([PT, NP, D]),
                                ALU.add).then_inc(pre_done, 1)
                v.tensor_tensor(sg[:, 1, :], SH[:, 0:I], sg[:, 0, :], ALU.subtract).then_inc(sh_lo, 1)
                v.tensor_tensor(sd[:, 1, :], SH[0:I, I:I + D], sd[:, 0, :], ALU.subtract).then_inc(sh_lo, 1)

            def maxima(step, i):
                b = num(back(step, 1))
                if i == 0:
                    until(dve, neg_made, b)
                dve.wait_ge(sm_done, b * (MT * NCH) + (i + 1))
                v.reduce_max(part_max[:, i // NCH, i % NCH:i % NCH + 1], SM[(back(step, 1)[1] + i) % 2][:, 0:CK],
                             axis=AX.X).then_inc(sm_maxed, 1)

            def body(step):
                for k in range(KT):
                    if on(step, 1) and 2 * k < MT * NCH:
                        maxima(step, 2 * k)
                    evacuate(step, k - 1)
                    if on(step, 3) and k == LAG:
                        b = num(back(step, 3))
                        dve.wait_ge(pv_done, b * KT + KT)
                        until(dve, nrm_done, b)
                        v.tensor_copy(o_raw[:, :], OB[:, 0:OC]).then_inc(o_copied, 1)
                    if on(step, 1) and 2 * k + 1 < MT * NCH:
                        maxima(step, 2 * k + 1)
                    if on(step, 3) and k - 1 == DEN_AT:
                        h, u = back(step, 3)
                        b = num((h, u))
                        v.reciprocal(o_rec[:, OC // 2:OC], EB[:, OC // 2:OC]).then_inc(rec_done, 1)
                        dve.wait_ge(rec_done, b * 2 + 2)
                        if u == 0:
                            until(dve, op_done, h)
                        v.tensor_tensor(o_nrm[:, :, u, :], o_raw[:, :].rearrange("p (n t) -> p n t", t=T),
                                        o_rec[:, :].rearrange("p (n t) -> p n t", t=T), ALU.mult).then_inc(nrm_done, 1)
                    if on(step, 1) and k == NEG_AT - 1:
                        b = num(back(step, 1))
                        dve.wait_ge(sm_maxed, b * (MT * NCH) + MT * NCH)
                        until(dve, neg_tr, b)
                        v.tensor_reduce(neg_max[:, :], part_max[:, :, :], axis=AX.X, op=ALU.max,
                                        negate=True).then_inc(neg_made, 1)

            def evacuate(step, k):
                c = k // TPC
                if k >= 0 and on(step, 0):
                    h, u = step
                    b = num(step)
                    if k % TPC == 0:
                        dve.wait_ge(ct_hi, b * NCH + (c + 1))
                        v.tensor_tensor(ctT[:, u, 1, c * CK:(c + 1) * CK], pj(step, "T", c)[:, 0:CK],
                                        ctT[:, u, 0, c * CK:(c + 1) * CK], ALU.subtract).then_inc(ct_lo, 1)
                    if k % TPC == 2:
                        dve.wait_ge(k_hi_done, b * NCH + (c + 1))
                        v.scalar_tensor_tensor(out=kparts[:, u, 1, c * CK:(c + 1) * CK],
                                               in0=pj(step, "K", c)[:, 0:CK], scalar=bkc[:, 0:1],
                                               in1=kparts[:, u, 0, c * CK:(c + 1) * CK],
                                               op0=ALU.add, op1=ALU.subtract).then_inc(k_lo_done, 1)
                    for at, i in PREP_AT[u]:
                        if at == k:
                            dve.wait_ge(w_hi_done, h * WPP + (i + 1))
                            v.tensor_tensor(w_out[:, i, 1:4:2, :], EB[:, 0:256].rearrange("p (a b) -> p a b", a=2),
                                            w_out[:, i, 0:4:2, :], ALU.subtract).then_inc(w_lo_done, 1)
                if on(step, 3) and k == DEN_AT:
                    b = num(back(step, 3))
                    dve.wait_ge(den_done, b + 1)
                    v.reciprocal(o_rec[:, 0:OC // 2], EB[:, 0:OC // 2]).then_inc(rec_done, 1)
                if on(step, 3) and k == OUT_AT and back(step, 3)[1] == 1:
                    h = back(step, 3)[0]
                    dve.wait_ge(op_done, h + 1)
                    v.scalar_tensor_tensor(out=xt[:, bass.ds(h, 1), :], in0=EB[0:PT, 0:D].unsqueeze(1),
                                           scalar=tg[:, 0:1], in1=xt[:, bass.ds(h, 1), :],
                                           op0=ALU.mult, op1=ALU.add).then_inc(x2_done, 1)

            attention(dve, body, B, {1: constant_term})

            dve.wait_ge(x2_done, NP)
            norm(2)
            for c in range(NTC):
                dve.wait_ge(xh_cp, c + 1)
                cols = slice(c * TC, (c + 1) * TC)
                v.tensor_copy(xnT[:, cols], bank[c][:, 0:TC]).then_inc(xf_cp, 1)
                v.tensor_tensor(q_lo[:, cols], bank[c][:, 0:TC], q_hi[:, cols], ALU.subtract).then_inc(xl_cp, 1)
            for q in range(6):
                n = min(3, NP - 3 * q)
                dve.wait_ge(lg_mm, q + 1)
                v.tensor_tensor(prob[:, 3 * q:3 * q + n, :],
                                bank[4 + q % 4][0:PT, 0:n * E].rearrange("p (n e) -> p n e", e=E),
                                eb_b[:, :].unsqueeze(1).to_broadcast([PT, n, E]), ALU.add).then_inc(lg_biased, 1)
            dve.wait_ge(prob_done, 1)
            for n in range(NP):
                v.max(top[:, n, :], prob[:, n, :]).then_inc(top_done, 1)
            for n in range(NP):
                dve.wait_ge(top_done, n + 1)
                v.match_replace(rep[:, n, :], top[:, n, :], prob[:, n, :], -1.0).then_inc(top_done, 1)
            link(v.reduce_sum(wsum[:, 0, :], top[:, :, :], axis=AX.X))
            link(v.tensor_scalar(wsum[:, 1, :], wsum[:, 0, :], EPS_TOPK, None, ALU.add))
            link(v.reciprocal(wsum[:, 2, :], wsum[:, 1, :]))
            dve.wait_ge(top_done, 2 * NP)
            link(v.scalar_tensor_tensor(out=comb, in0=rep, scalar=0.0, in1=prob, op0=ALU.is_lt, op1=ALU.mult))
            link(v.tensor_tensor(comb, comb, wsum[:, 2, :].unsqueeze(2).to_broadcast([PT, NP, E]), ALU.mult))
            v.tensor_scalar(comb, comb, ROUTED_SCALE, None, ALU.mult).then_inc(comb_done, 1)
            g4 = comb.rearrange("p n (g e) -> p n g e", g=EG)
            dve.wait_ge(part_cast, 1)
            v.tensor_tensor(g4, g4, parts[:, :, :, 0:GE], ALU.subtract).then_inc(part_rest, 1)
            dve.wait_ge(part_cast, 2)
            v.tensor_tensor(parts[:, :, :, 2 * GE:3 * GE], g4, parts[:, :, :, GE:2 * GE], ALU.subtract)\
                .then_inc(parts_done, 1)

            for t in range(NTC):
                dve.wait_ge(hh_done, t + 1)
                v.tensor_tensor(h_lo[0:I, t, :], h_f[0:I, t, :], h_hi[0:I, t, :], ALU.subtract).then_inc(hl_done, 1)

            def weigh(n, t, first=False):
                m = n * NTC + (NTC + t)
                dve.wait_ge(s_done, m + 1)
                dve.wait_ge(c_done, n * NTC + (t + 1))
                dve.wait_ge(hh_done, m - (NTC - 1))
                v.tensor_tensor(h_f[:, t, :], CB[t % 2][:, 0:TC], s_act[:, t % 2, :], ALU.mult).then_inc(h_done, 1)

            def lo_part(n, t):
                dve.wait_ge(hh_done, n * NTC + (NTC + t + 1))
                v.tensor_tensor(h_lo[:, t, :], h_f[:, t, :], h_hi[:, t, :], ALU.subtract).then_inc(hl_done, 1)

            def pairs(base, first=False):
                for q in range(WR):
                    for t in range(NTC):
                        weigh(base + q, t)
                        if t:
                            lo_part(base + q, t - 1)
                        elif not (first and q == 0):
                            lo_part(base + (q - 1), NTC - 1)

            pairs(0, True)
            with dve.Fori(1, EP // WR) as i:
                pairs(i * WR)
            lo_part(EP - 1, NTC - 1)
            for c in range(NTC):
                dve.wait_ge(y_tr, c + 1)
                v.scalar_tensor_tensor(out=xc[:, c * PPC:(c + 1) * PPC, :],
                                       in0=bank[4 + c][0:PT, :].rearrange("p (n c) -> p n c", c=D),
                                       scalar=tg[:, 1:2], in1=xt[:, c * PPC:(c + 1) * PPC, :],
                                       op0=ALU.mult, op1=ALU.add).then_inc(fin_done, 1)

        @block.tensor
        def _(pe):
            pe.wait_ge(consts, IDENT)
            pe.wait_ge(weights_in, 16 * 4)
            for n in range(4):
                pe.transpose(bank[n][:, 0:D], w_raw[:, n, :], ident[:, :]).then_inc(wp_tr, 1)

            def transpose_tokens(c):
                for i in range(PPC):
                    last = pe.transpose(bank[c][:, i * PT:(i + 1) * PT], xc[:, c * PPC + i, :], ident[0:PT, 0:PT])
                last.then_inc(xn_tr, 1)

            pe.wait_ge(ln_done, 1)
            pe.wait_ge(wp_cp, 4)
            pe.wait_ge(wp_lo, 2)
            for c in range(NTC):
                transpose_tokens(c)
            for c in range(NTC):
                pe.wait_ge(xn_cp, c + 1)
                pe.matmul(bank[c][:, 0:TC], wqT[:, :], xnT[:, c * TC:(c + 1) * TC], start=True, stop=True)\
                  .then_inc(q_mm, 1)

            def shared_and_router():
                pe.wait_ge(late_in, 16 * 3)
                pe.transpose(SH[:, 0:I], sh_raw[0:I, 0, :], ident[0:I, 0:I]).then_inc(sh_tr, 1)
                pe.transpose(SH[0:I, I:I + D], sh_raw[:, 1, 0:I], ident[:, :]).then_inc(sh_tr, 1)
                for a in range(2):
                    last = pe.transpose(SH[:, I + D + a * (E // 2):I + D + (a + 1) * (E // 2)], r_raw[:, a, :],
                                        ident[0:E // 2, 0:E // 2])
                last.then_inc(sh_tr, 1)
                pe.wait_ge(bv_made, 1)
                pe.matmul(SH[0:PT, I + D + E:I + 2 * D + E], bv_rep[:, :], woT[:, :], start=True, stop=True)\
                  .then_inc(cv_mm, 1)
                pe.wait_ge(q_hi_done, NTC)
                pe.wait_ge(q_lo_done, NTC)
                pe.wait_ge(consts, MASKS)

            def before_values():
                pe.wait_ge(consts, K_ONES)
                pe.wait_ge(sh_cp, 3)
                pe.wait_ge(sh_lo, 2)
                pe.wait_ge(pre_done, 1)
                pe.wait_ge(wo_rows, 16 * H)

            def value_product(bt, j):
                h, u = bt
                b = num(bt)
                pe.wait_ge(exp_done, b * (2 * KT) + (2 * j + 2))
                if j % TPC == 0:
                    pe.wait_ge(v_copied, b * NCH + (j // TPC + 1))
                if j == 0:
                    until(pe, o_copied, b)
                for g in range(VG):
                    at, w = (0, VC) if g < 4 else (VC, T)
                    src = VC * g if g < 4 else 4 * VC + T * (g - 4)
                    last = pe.matmul(OB[32 * (g % 4):32 * (g % 4) + 32, at:at + w],
                                     v_sb[:, u, j, g, :], p_exp[0:KP, j % PR, src:src + w],
                                     start=(j == 0 and g < 4), stop=(j == KT - 1), skip_group_check=True)
                last.then_inc(pv_done, 1)

            def scores(bt, j, f):
                h, u = bt
                b = num(bt)
                if j == 0 and f == 0:
                    pe.wait_ge(kst_here[u], h * (16 * 3 * HG) + 16 * 3 * HG)
                    pe.wait_ge(row_here[u], h * 16 + 16)
                until(pe, exp_done, b * (2 * KT) + (2 * j + f - 1))
                for g in (2 * f, 2 * f + 1):
                    last = pe.matmul(ST[f][0:KP, (g % 2) * GC:(g % 2 + 1) * GC],
                                     k_stk[0:97, u, g, j * KP:(j + 1) * KP],
                                     q_st[0:97, u, g, :, :].rearrange("p a t -> p (a t)"), start=True, stop=True)
                last.then_inc(st_done, 1)

            def maxima(step, i):
                u = back(step, 1)[1]
                b = num(back(step, 1))
                m, c = i // NCH, i % NCH
                if i == 0:
                    pe.wait_ge(qblk_made, b + 1)
                    pe.wait_ge(k_hi_done, b * NCH + NCH)
                until(pe, sm_maxed, b * (MT * NCH) + (i - 1))
                rows = q_blk[:, u, :, :].rearrange("p a t -> p (a t)")[:, 128 * m:128 * m + 128]
                pe.matmul(SM[(u + i) % 2][:, 0:CK], rows, kparts[:, u, 0, c * CK:(c + 1) * CK],
                          start=True, stop=True).then_inc(sm_done, 1)

            def body(step):
                for k in range(KT):
                    js, bs, scores_there = tile_at(step, k, 0)
                    jv, bv_, values_there = tile_at(step, k, 1)
                    for f in range(2):
                        if scores_there:
                            scores(bs, js, f)
                        if f == 0 and on(step, 1) and 2 * k < MT * NCH:
                            maxima(step, 2 * k)
                    if values_there:
                        value_product(bv_, jv)
                    if on(step, 1) and 2 * k + 1 < MT * NCH:
                        maxima(step, 2 * k + 1)
                    c = k // TPC
                    if on(step, 0):
                        h, u = step
                        b = num(step)
                        if k % TPC == 0:
                            if c == 0:
                                pe.wait_ge(ctx_here[u], h * 16 + 16)
                            until(pe, k_hi_done, b * NCH + c)
                            until(pe, k_lo_done, b * NCH + c)
                            for i in range(TPC):
                                last = pe.transpose(pj(step, "T", c)[:, i * KP:(i + 1) * KP],
                                                    ctx_in[:, u, c * TPC + i, :], ident[0:KP, 0:KP])
                            last.then_inc(t_done, 1)
                        if k % TPC == 2:
                            pe.wait_ge(ct_lo, b * NCH + (c + 1))
                            until(pe, v_copied, (b - 1) * NCH + c)
                            for i, (w, part) in enumerate(((wk_hi, 0), (wk_lo, 0), (wk_hi, 1))):
                                last = pe.matmul(pj(step, "K", c)[:, 0:CK], w[:, :],
                                                 ctT[:, u, part, c * CK:(c + 1) * CK], start=(i == 0), stop=(i == 2))
                            last.then_inc(kp_done, 1)
                    if on(step, 1) and k % TPC == 3:
                        u = back(step, 1)[1]
                        b = num(back(step, 1))
                        if on(step, 0):
                            pe.wait_ge(ct_lo, (b + 1) * NCH + (c + 1))
                        else:
                            pe.wait_ge(k_lo_done, (b + 1) * NCH)
                            pe.wait_ge(v_copied, b * NCH + c)
                        for i in range(TPC):
                            cols = slice((c * TPC + i) * KP, (c * TPC + i + 1) * KP)
                            for n, (part, w) in enumerate(((0, wv_hi), (0, wv_lo), (1, wv_hi))):
                                last = pe.matmul(pj(step, "V", c)[0:KP, i * D:(i + 1) * D], ctT[:, u, part, cols],
                                                 w[:, :], start=(n == 0), stop=(n == 2))
                        last.then_inc(vp_done, 1)
                    if on(step, 0):
                        h, u = step
                        for n, (at, i) in enumerate(PREP_AT[u]):
                            if at == k:
                                pe.wait_ge(w_here[i], h * 32 + 32)
                                until(pe, w_lo_done, h * WPP + i)
                                if n == 0:
                                    until(pe, neg_copied, num(back(step, 1)))
                                if at > DEN_AT and on(step, 3):
                                    pe.wait_ge(rec_done, num(back(step, 3)) * 2 + 2)
                                for a in range(2):
                                    last = pe.transpose(EB[:, a * 128:(a + 1) * 128], w_in[:, i, a, :], ident[:, :])
                                last.then_inc(w_tr, 1)
                    if on(step, 3) and k == DEN_AT:
                        b = num(back(step, 3))
                        if on(step, 0):
                            done = [i for at, i in PREP_AT[step[1]] if at < DEN_AT][-1]
                            pe.wait_ge(w_lo_done, step[0] * WPP + (done + 1))
                        else:
                            pe.wait_ge(neg_copied, min(num(back(step, 1)), B))
                            pe.wait_ge(w_lo_done, EP)
                            pe.wait_ge(x2_done, b // 2)
                        pe.wait_ge(o_copied, b + 1)
                        pe.matmul(EB[:, 0:OC], den_pick[:, :], o_raw[:, :], start=True, stop=True)\
                          .then_inc(den_done, 1)
                    if on(step, 3) and k == OUT_AT and back(step, 3)[1] == 1:
                        h = back(step, 3)[0]
                        if on(step, 0):
                            pe.wait_ge(w_lo_done, step[0] * WPP + (PREP_AT[step[1]][-1][1] + 1))
                        pe.wait_ge(nrm_done, h * 2 + 2)
                        for n in range(4):
                            last = pe.matmul(EB[0:PT, 0:D], o_nrm[:, n, :, :].rearrange("p a t -> p (a t)"),
                                             wo_m[:, n, :], start=(n == 0), stop=(n == 3))
                        last.then_inc(op_done, 1)
                    if on(step, 1) and k == NEG_AT:
                        b = num(back(step, 1))
                        if on(step, 0):
                            pe.wait_ge(w_lo_done, step[0] * WPP + (PREP_AT[step[1]][-1][1] + 1))
                        if on(step, 3):
                            pe.wait_ge(rec_done, num(back(step, 3)) * 2 + 2)
                            if back(step, 3)[1] == 1:
                                pe.wait_ge(x2_done, back(step, 3)[0] + 1)
                        pe.wait_ge(neg_made, b + 1)
                        pe.transpose(EB[0:MT, 0:64].bitcast(fp16), neg_max[:, :], ident16[:, :]).then_inc(neg_tr, 1)

            attention(pe, body, B, {1: shared_and_router, 2: before_values})

            pe.wait_ge(consts, NCONST)
            pe.wait_ge(ln_done, 2)
            for c in range(NTC):
                transpose_tokens(c)
            pe.wait_ge(x2_done, NP)
            for q in range(6):
                n = min(3, NP - 3 * q)
                pe.wait_ge(xf_cp, min(NTC, (3 * q + n - 1) // PPC + 1))
                if q >= 4:
                    pe.wait_ge(lg_biased, q - 3)
                for i in range(n):
                    last = pe.matmul(bank[4 + q % 4][0:PT, i * E:(i + 1) * E],
                                     xnT[:, (3 * q + i) * PT:(3 * q + i + 1) * PT], rT[:, :], start=True, stop=True)
                last.then_inc(lg_mm, 1)
            pe.wait_ge(parts_done, 1)
            for n in range(NP):
                if n >= 4:
                    pe.wait_ge(cb_cp, n - 3)
                out_b = bank[4 + n % 4][0:PW, 0:EG * PT // 2].bitcast(bf16)
                for g in range(EG):
                    last = pe.transpose(out_b[:, g * PT:(g + 1) * PT], parts[:, n, g, :], identb[0:PT, 0:PT])
                last.then_inc(cb_tr, 1)
            pe.wait_ge(cb_cp, NP)
            pe.wait_ge(xl_cp, NTC)

            hilo = ((0, 0), (1, 0), (0, 1))
            xparts = (q_hi, q_lo)
            hparts = (h_hi, h_lo)
            for t in range(NTC):
                if t >= 2:
                    pe.wait_ge(s_done, t - 1)
                for i, (a, b) in enumerate(hilo):
                    last = pe.matmul(ZB[t % 2][0:I, 0:TC], sg[:, a, :], xparts[b][:, t * TC:(t + 1) * TC],
                                     start=(i == 0), stop=(i == 2))
                last.then_inc(z_done, 1)

            def down(n, t, q, shared=False, end=False):
                pe.wait_ge(hl_done, n * NTC + (NTC + t + 1))
                for i, (a, b) in enumerate(hilo):
                    rows = slice(0, I if shared else 128)
                    w = sd[:, a, :] if shared else w_ring[:, q, 2 + a, :]
                    last = pe.matmul(YB[t][:, 0:TC], w, hparts[b][rows, t, :], start=(shared and i == 0),
                                     stop=(end and i == 2), skip_group_check=True)
                last.then_inc(dn_done, 1)

            def pairs(i, g, first=False):
                for q in range(WR):
                    n = i * WR + q
                    for t in range(NTC):
                        m = n * NTC + (NTC + t)
                        down(n - 1, t, (q - 1) % WR, shared=first and q == 0)
                        if t == 0:
                            pe.wait_ge(ring_here[q], i * 16 + 16)
                        pe.wait_ge(s_done, m - 1)
                        for j, (a, b) in enumerate(hilo):
                            last = pe.matmul(ZB[t % 2][:, 0:TC], w_ring[:, q, a, :], xparts[b][:, t * TC:(t + 1) * TC],
                                             start=(j == 0), stop=(j == 2))
                        last.then_inc(z_done, 1)
                        if not (first and q == 0 and t < 2):
                            pe.wait_ge(h_done, m - (NTC + 1))
                        at = (n - g * GP) * 128
                        pe.matmul(CB[t % 2][:, 0:TC], expand[0:PW, :, :].rearrange("p e i -> p (e i)")[:, bass.ds(at, 128)],
                                  combT[0:PW, g, t * TC:(t + 1) * TC], start=True, stop=True).then_inc(c_done, 1)

            pairs(0, 0, True)
            for g in range(EG):
                with pe.Fori(g * GP // WR + (1 if g == 0 else 0), (g + 1) * GP // WR) as i:
                    pairs(i, g)
            for t in range(NTC):
                down(EP - 1, t, WR - 1, end=True)
            for c in range(NTC):
                pe.wait_ge(y_cp, c + 1)
                for i in range(PPC):
                    last = pe.transpose(bank[4 + c][0:PT, i * D:(i + 1) * D],
                                        xnT[:, (c * PPC + i) * PT:(c * PPC + i + 1) * PT], ident[:, :])
                last.then_inc(y_tr, 1)


_INS = ['x', 'ctx_1024', 'g_xattn', 'g_ffn', 'L0_xattn_Wq', 'L0_xattn_bq', 'L0_xattn_Wk', 'L0_xattn_bk',
        'L0_xattn_Wv', 'L0_xattn_bv', 'L0_xattn_Wo', 'L0_xattn_bo', 'L0_ffn_router_w', 'L0_ffn_expert_bias',
        'L0_ffn_w_gate', 'L0_ffn_w_down', 'L0_ffn_w_gate_shared', 'L0_ffn_w_down_shared']
_OUTS = [((32, 56, 128), 'float32')]


def kernel(**inputs):
    import numpy as _np
    import concourse.bacc as _bacc
    from concourse import mybir as _mybir
    from concourse.bass_utils import run_bass_kernel_spmd as _run

    nc = _bacc.Bacc("TRN2", target_bir_lowering=False, num_devices=1)
    arrays, args = {}, []
    for name in _INS:
        a = _np.ascontiguousarray(inputs[name])
        arrays[f"in_{name}_dram"] = a
        args.append(nc.dram_tensor(f"in_{name}_dram", a.shape, _mybir.dt.from_np(a.dtype), kind="ExternalInput").ap())
    for i, (shape, dtype) in enumerate(_OUTS):
        dt = _mybir.dt.from_np(_np.dtype(dtype))
        args.append(nc.dram_tensor(f"out_{i}_dram", shape, dt, kind="ExternalOutput").ap())
    flamingo_gated_block(nc, *args)
    r = _run(nc, [arrays], core_ids=[0])
    got = tuple(r.results[0][f"out_{i}_dram"] for i in range(len(_OUTS)))
    return got[0]
```

```python
import concourse.bass as bass
from concourse import mybir
from contextlib import ExitStack


def flamingo_gated_block(nc, x, ctx, g_xattn, g_ffn, Wq, bq, Wk, bk, Wv, bv, Wo, bo,
                         router_w, expert_bias, w_gate, w_down, w_gate_shared, w_down_shared, out):
    fp32 = mybir.dt.float32
    fp16 = mybir.dt.float16
    ALU = mybir.AluOpType
    ACT = mybir.ActivationFunctionType
    AX = mybir.AxisListType

    B, T, D = x.shape
    C = ctx.shape[1]
    H = 16
    d = D // H
    E, I, _ = w_gate.shape
    TOP_K = 8
    ROUTED_SCALE = 2.5
    EPS_LN = 1e-5
    EPS_TOPK = 1e-9
    QSCALE = float(d) ** -0.5

    N = B * T
    PT = 2 * T
    NP = B // 2
    HT = H * T
    KT = 12
    KP = C // KT
    NCH = 3
    CK = C // NCH
    TPC = KT // NCH
    MT = HT // 128
    HG = 4
    GC = HT // HG
    VG = 8
    VC = 3 * T
    OC = 4 * T
    PR = 3
    NTC = 4
    TC = N // NTC
    PPC = NP // NTC
    EP = E // 2
    WPP = EP // (B // 2)
    WR = 4
    LAG = 3
    PREP_AT = {0: [(1, 0), (3, 1), (8, 2)], 1: [(3, 3), (8, 4)]}
    DEN_AT, SPREAD_AT, OUT_AT, NEG_AT = 5, 7, 10, KT - 1
    EARLY, LATE = (0, 12), (12, NP)
    FIRST, REST = (0, PPC), (PPC, NP)
    CENTRE_REST_AT, VAR_REST_AT, SCALE_REST_AT, TOKENS_REST_AT, Q_REST_AT = (0, 3), (0, 4), (0, 5), (0, 7), (0, 9)
    CONSTANT_AT, BANK_FREE_AT = (1, 11), (2, 1)
    CENTRE_AT, VAR_AT, SCALE_AT = (B, 0), (B, 2), (B, 3)
    TOKENS_AT = {(B, 5): 0, (B, 9): 1, (B + 1, 0): 2}
    LOGITS_AT = {(B + 1, 1): (0, 1), (B + 1, 2): (2, 3)}
    PROB_AT, TOP_AT, COMB_AT = (B + 1, 3), (B + 1, 4), (B + 1, 8)
    COMBT_AT = {(B + 1, 11): 0, (B + 2, 0): 1, (B + 2, 1): 2}

    stk = ExitStack()
    with stk:
        def sb(name, shape, dt=fp32):
            return stk.enter_context(nc.sbuf_tensor(name, shape, dt))

        def sem(name):
            return stk.enter_context(nc.semaphore(name))

        ident = sb("ident", [128, 128])
        ident16 = sb("ident16", [128, 128], fp16)
        head_mask = sb("head_mask", [128, H], fp16)
        stack_mask = sb("stack_mask", [96, HG], fp16)
        den_pick = sb("den_pick", [128, 4])
        ones_d = sb("ones_d", [D, PT])
        w_raw = sb("w_raw", [128, 4, D])
        wqT = sb("wqT", [D, D])
        woT = sb("woT", [D, D])
        wk_hi = sb("wk_hi", [D, D], fp16)
        wk_lo = sb("wk_lo", [D, D], fp16)
        wv_hi = sb("wv_hi", [D, D], fp16)
        wv_lo = sb("wv_lo", [D, D], fp16)
        wo_m = sb("wo_m", [128, 4, D])
        bqc = sb("bqc", [D, 1])
        bqs = sb("bqs", [D, 1])
        bkc = sb("bkc", [D, 1])
        bvc = sb("bvc", [D, 1])
        bv_rep = sb("bv_rep", [D, PT])
        bo_b = sb("bo_b", [PT, D])
        eb_b = sb("eb_b", [PT, E])
        g_raw = sb("g_raw", [PT, 2])
        tg = sb("tg", [PT, 2])
        xt = sb("xt", [PT, NP, D])
        xc = sb("xc", [PT, NP, D])
        stat = sb("stat", [PT, 5, NP])
        xnT = sb("xnT", [D, N])
        q_hi = sb("q_hi", [D, N], fp16)
        q_lo = sb("q_lo", [D, N], fp16)
        q_stk = sb("q_stk", [128, HG, N], fp16)
        ctx_in = sb("ctx_in", [KP, 2, KT, D])
        ctT = sb("ctT", [D, 2, 2, C], fp16)
        kparts = sb("kparts", [D, 2, 2, C], fp16)
        k_stk = sb("k_stk", [128, 2, HG, C], fp16)
        v_sb = sb("v_sb", [128, 2, KT, VG, 32])
        q_blk = sb("q_blk", [D, 2, H, T], fp16)
        q_st = sb("q_st", [128, 2, HG, HG, T], fp16)
        part_max = sb("part_max", [128, MT, NCH])
        neg_max = sb("neg_max", [128, MT], fp16)
        neg_row = sb("neg_row", [MT, 128], fp16)
        p_exp = sb("p_exp", [128, PR, HT])
        o_raw = sb("o_raw", [128, OC])
        rec = sb("rec", [PT, 2, 4])
        rec_wide = sb("rec_wide", [PT, 2, 128])
        o_nrm = sb("o_nrm", [128, 4, 2, T])
        w_in = sb("w_in", [128, WPP, 2, 128])
        w_out = sb("w_out", [128, WPP, 4, 128], fp16)
        w_ring = sb("w_ring", [128, WR, 4, 128], fp16)
        sh_raw = sb("sh_raw", [128, 2, D])
        sg = sb("sg", [128, 2, I], fp16)
        sd = sb("sd", [I, 2, D], fp16)
        r_raw = sb("r_raw", [E // 2, 2, D])
        rT = sb("rT", [D, E])
        top = sb("top", [PT, NP, TOP_K])
        wsum = sb("wsum", [PT, 3, NP])
        c_scratch = nc.dram_tensor("c_scratch", [EP, 2, N], fp32, kind="Internal").ap()
        w_scratch = nc.dram_tensor("w_scratch", [EP, 128, 4, 128], fp16, kind="Internal").ap()

        def flat(ap, pattern, dt=None):
            a = ap.rearrange(pattern)
            return a.bitcast(dt) if dt is not None else a

        k_words = flat(kparts[:, :, :, :], "p a b c -> p (a b c)", fp32)
        e_words = flat(p_exp[:, :, :], "p a b -> p (a b)")
        sq_rest = e_words[0:PT, 0:(NP - PPC) * D].rearrange("p (n c) -> p n c", c=D)
        sq_first = e_words[0:PT, (NP - PPC) * D:NP * D].rearrange("p (n c) -> p n c", c=D)
        q_tmp = e_words[:, NP * D:NP * D + TC]
        sq_early = xnT[0:PT, 0:EARLY[1] * D].rearrange("p (n c) -> p n c", c=D)
        sq_late = flat(w_in[0:PT, :, :, :], "p a b c -> p (a b c)")[:, 0:(NP - LATE[0]) * D]\
            .rearrange("p (n c) -> p n c", c=D)
        prob = k_words[0:PT, 0:NP * E].rearrange("p (n e) -> p n e", e=E)
        c_words = flat(ctx_in[:, :, :, :], "p a b c -> p (a b c)")
        comb = c_words[0:PT, 0:NP * E].rearrange("p (n e) -> p n e", e=E)
        combT = flat(q_stk[:, :, :], "p a b -> p (a b)", fp32)\
            .rearrange("p (a t) -> p a t", a=2)
        h_words = flat(k_stk[:, :, :, :], "p a b c -> p (a b c)", fp32)
        h_f = h_words[:, 0:N].rearrange("p (a t) -> p a t", a=NTC)
        v_words = flat(v_sb[:, :, :, :, :], "p a b c e -> p (a b c e)")
        c_ring = [v_words[:, i * N:(i + 1) * N] for i in range(WR - 1)] + [h_words[:, N:2 * N]]
        t_words = flat(ctT[:, :, :, :], "p a b c -> p (a b c)")
        h_hi = t_words[:, 0:N].rearrange("p (a t) -> p a t", a=NTC)
        h_lo = t_words[:, N:2 * N].rearrange("p (a t) -> p a t", a=NTC)
        s_act = t_words[:, 2 * N:2 * N + 4 * TC].bitcast(fp32).rearrange("p (a t) -> p a t", a=2)

        bank = [stk.enter_context(nc.psum_tensor(f"bank{i}", [128, 512], fp32)) for i in range(8)]
        ST = [bank[0], bank[1]]
        SM = [bank[2], bank[3]]
        OB = bank[4]
        PJ = [bank[5], bank[6]]
        EB = bank[7]
        SH = bank[4]
        YB = [bank[0], bank[1], bank[2], bank[3]]
        ZB = [bank[4], bank[5], bank[6], bank[7]]
        TOKB = [PJ[1], PJ[1], PJ[1], bank[2]]
        LGB = [bank[2], bank[3], bank[5], bank[6], bank[3], bank[0]]
        CTB = [bank[2], bank[3], bank[5], bank[6], bank[2], bank[3], bank[1], bank[2]]

        names = """consts weights_in bias_in small_in late_in x_in x_rest wp_tr wp_cp wp_lo
            ln_sub ln_sq ln_var ln_root table_loaded ln_done xn_tr xn_cp bqs_made gates_made bv_made
            q_mm q_hi_done q_lo_done q_rows wo_rows cv_mm constant_made pre_done sh_tr sh_cp sh_lo o_cleared
            t_done ct_hi ct_lo kp_done k_hi_done k_lo_done vp_done v_copied qblk_made qst_made
            sm_done sm_maxed neg_made neg_tr neg_copied st_done exp_done pv_done o_copied den_done rec_done wide_done spread_done
            nrm_done op_done x2_done w_tr w_hi_done w_lo_done
            xf_cp xh_cp xl_cp lg_mm lg_biased prob_done top_done comb_done cb_tr cb_cp c_stored
            z_done s_done h_done hh_done hl_done dn_done y_cp y_tr fin_done stored dve_chain""".split()
        S = {name: sem(name) for name in names}
        (consts, weights_in, bias_in, small_in, late_in, x_in, x_rest, wp_tr, wp_cp, wp_lo,
         ln_sub, ln_sq, ln_var, ln_root, table_loaded, ln_done, xn_tr, xn_cp, bqs_made, gates_made, bv_made,
         q_mm, q_hi_done, q_lo_done, q_rows, wo_rows, cv_mm, constant_made, pre_done, sh_tr, sh_cp, sh_lo, o_cleared,
         t_done, ct_hi, ct_lo, kp_done, k_hi_done, k_lo_done, vp_done, v_copied, qblk_made, qst_made,
         sm_done, sm_maxed, neg_made, neg_tr, neg_copied, st_done, exp_done, pv_done, o_copied, den_done, rec_done, wide_done, spread_done,
         nrm_done, op_done, x2_done, w_tr, w_hi_done, w_lo_done,
         xf_cp, xh_cp, xl_cp, lg_mm, lg_biased, prob_done, top_done, comb_done, cb_tr, cb_cp, c_stored,
         z_done, s_done, h_done, hh_done, hl_done, dn_done, y_cp, y_tr, fin_done, stored, dve_chain) = \
            [S[name] for name in names]
        ctx_here = [sem(f"ctx_here{i}") for i in range(2)]
        kst_here = [sem(f"kst_here{i}") for i in range(2)]
        row_here = [sem(f"row_here{i}") for i in range(2)]
        w_here = [sem(f"w_here{i}") for i in range(WPP)]
        w_stored = [sem(f"w_stored{i}") for i in range(WPP)]
        c_here = [sem(f"c_here{i}") for i in range(WR)]
        ring_here = [sem(f"ring_here{i}") for i in range(WR)]
        IDENT, MASKS, V_ONES, K_ONES = 2, 11, 12, 13
        NSMALL = 4
        QROWS = 2 * 16 * 3 * HG

        def back(hu, n):
            v = hu[1] - n
            return (hu[0] + v // 2, v % 2)

        def num(hu):
            return hu[0] * 2 + hu[1]

        def on(step, n):
            return not isinstance(step[0], int) or 0 <= num(step) - n < B

        def until(eng, s, value):
            if not isinstance(value, int) or value > 0:
                eng.wait_ge(s, value)

        def attention(eng, body, loop_to=B, before={}):
            for s in range(4):
                if s in before:
                    before[s]()
                body((s // 2, s % 2))
            with eng.Fori(2, loop_to // 2) as h:
                body((h, 0))
                body((h, 1))
            for s in range(loop_to, B + 3):
                body((s // 2, s % 2))

        def aside(step, k, *stages):
            for at, stage in stages:
                if isinstance(step[0], int) and (num(step), k) == at:
                    stage()

        def chunks_at(k, place):
            i = 2 * k + place
            return [i] if i < MT * NCH else []

        def tile_at(step, k, late):
            j = k - LAG - late
            return (j, back(step, 2), on(step, 2)) if j >= 0 else (j + KT, back(step, 3), on(step, 3))

        def pj(step, kind, c):
            return PJ[(step[1] + 3 * c + "TKV".index(kind)) % 2]

        def row(ap):
            return ap.rearrange("(a n) -> a n", a=1)

        gate_pairs = w_gate.rearrange("(n e) i h -> n (e i) h", e=2)
        down_pairs = w_down.rearrange("(n e) h i -> n h e i", e=2)

        block = stk.enter_context(nc.Block())

        @block.sync
        def _(sp):
            def load_x(p0, p1, here):
                for b in range(2):
                    sp.dma_start(xt[b * T:(b + 1) * T, p0:p1, :],
                                 x.rearrange("(n b) t c -> b t n c", b=2)[b, :, p0:p1, :]).then_inc(here, 16)

            load_x(*FIRST, x_in)
            for n, w in enumerate((Wq, Wk, Wv, Wo)):
                sp.dma_start(w_raw[:, n, :], w).then_inc(weights_in, 16)
            for dst, src in ((bqc, bq), (bkc, bk), (bvc, bv)):
                sp.dma_start(dst[:, :], src.rearrange("(p a) -> p a", a=1)).then_inc(bias_in, 16)
            sp.dma_start(ctx_in[:, 0, :, :], ctx[0].rearrange("(p j) c -> p j c", j=KT)).then_inc(ctx_here[0], 16)
            load_x(*REST, x_rest)
            sp.dma_start(bo_b[:, :], row(bo).to_broadcast([PT, D])).then_inc(small_in, 16)
            sp.dma_start(eb_b[:, :], row(expert_bias).to_broadcast([PT, E])).then_inc(small_in, 16)
            for n, g in enumerate((g_xattn, g_ffn)):
                sp.dma_start(g_raw[:, n:n + 1], row(g).to_broadcast([PT, 1])).then_inc(small_in, 16)
            sp.dma_start(ctx_in[:, 1, :, :], ctx[1].rearrange("(p j) c -> p j c", j=KT)).then_inc(ctx_here[1], 16)
            sp.dma_start(sh_raw[0:I, 0, :], w_gate_shared).then_inc(late_in, 16)
            sp.dma_start(sh_raw[:, 1, 0:I], w_down_shared).then_inc(late_in, 16)
            sp.dma_start(r_raw[:, :, :], router_w.rearrange("(a p) h -> p a h", a=2)).then_inc(late_in, 16)
            def stack_queries(c0, c1):
                sp.wait_ge(q_hi_done, c1)
                sp.wait_ge(q_lo_done, c1)
                cols = slice(c0 * TC, c1 * TC)
                for g in range(HG):
                    for r, part in enumerate((q_hi, q_lo, q_hi)):
                        sp.dma_start(q_stk[32 * r:32 * r + 32, g, cols], part[32 * g:32 * g + 32, cols])\
                          .then_inc(q_rows, 16)

            stack_queries(0, 1)
            sp.wait_ge(wp_cp, 4)
            sp.wait_ge(o_cleared, 1)
            for h in range(H):
                g, c = (h // 3, h % 3) if h < 12 else (h - 12, 3)
                p0 = 32 * g + (d * c if c < 3 else 0)
                sp.dma_start(wo_m[p0:p0 + d, c, :], woT[d * h:d * h + d, :]).then_inc(wo_rows, 16)
            stack_queries(1, NTC)

            def body(step):
                if on(step, 1):
                    h, u = back(step, 1)
                    b = num((h, u))
                    read, made = (b - 1) * (2 * KT), b * NCH + NCH
                    if not isinstance(h, int):
                        read, made = sp.to_reg(read), sp.to_reg(made)
                    until(sp, st_done, read)
                    sp.wait_ge(k_lo_done, made)
                    for g in range(HG):
                        for r, part in enumerate((0, 0, 1)):
                            sp.dma_start(k_stk[32 * r:32 * r + 32, u, g, :], kparts[32 * g:32 * g + 32, u, part, :])\
                              .then_inc(kst_here[u], 16)
                if on(step, -1) and not (isinstance(step[0], int) and num(step) < 1):
                    h, u = back(step, -1)
                    b = num((h, u))
                    sp.wait_ge(t_done, (b - 1) * NCH)
                    sp.dma_start(ctx_in[:, u, :, :], ctx[bass.ds(b, 1)].rearrange("a (p j) c -> p (a j) c", j=KT))\
                      .then_inc(ctx_here[u], 16)
                if on(step, 1):
                    u = back(step, 1)[1]
                    b = num(back(step, 1))
                    sp.wait_ge(qst_made, b + 1)
                    sp.wait_ge(neg_copied, b + 1)
                    sp.dma_start(q_st[96:97, u, :, :, :].rearrange("p a b c -> p (a b c)"), neg_row[:, :])\
                      .then_inc(row_here[u], 16)

            attention(sp, body, B - 2)

            for i in range(WPP):
                sp.wait_ge(w_stored[i], 16 * (B // 2))
            for n in range(WR):
                sp.dma_start(w_ring[:, n, :, :], w_scratch[n]).then_inc(ring_here[n], 16)
            def weights_of(n, q, t0=0, t1=N):
                for a in range(2):
                    src = c_scratch[n:n + 1, a, t0:t1] if isinstance(n, int) else \
                        c_scratch[bass.ds(n, 1)].rearrange("o a t -> o (a t)")[:, a * N:(a + 1) * N]
                    sp.dma_start(c_ring[q][a * I:(a + 1) * I, t0:t1], src.to_broadcast([I, t1 - t0]))\
                      .then_inc(c_here[q], 16)

            for c0, c1 in ((0, NTC - 1), (NTC - 1, NTC)):
                for c in range(c0, c1):
                    sp.wait_ge(cb_cp, 2 * c + 2)
                    sp.dma_start(c_scratch[:, :, c * TC:(c + 1) * TC], combT[0:EP, :, c * TC:(c + 1) * TC])\
                      .then_inc(c_stored, 16)
                sp.wait_ge(pv_done, B * KT)
                sp.wait_ge(c_stored, 16 * c1)
                for n in range(WR):
                    weights_of(n, n, c0 * TC, c1 * TC)
            with sp.Fori(1, EP // WR) as i:
                for q in range(WR):
                    used = sp.to_reg(i * (WR * NTC) + (q - WR + 2) * NTC)
                    weighed = sp.to_reg(i * (WR * NTC) + (q - WR + 1) * NTC)
                    sp.wait_ge(dn_done, used)
                    sp.dma_start(w_ring[:, q, :, :], w_scratch[bass.ds(i * WR + q, 1)].rearrange("a p b c -> p (a b) c"))\
                      .then_inc(ring_here[q], 16)
                    sp.wait_ge(h_done, weighed)
                    weights_of(i * WR + q, q)
            for c in range(NTC):
                sp.wait_ge(fin_done, c + 1)
                for b in range(2):
                    sp.dma_start(out.rearrange("(n b) t c -> b t n c", b=2)[b, :, c * PPC:(c + 1) * PPC, :],
                                 xc[b * T:(b + 1) * T, c * PPC:(c + 1) * PPC, :]).then_inc(stored, 16)
            sp.wait_ge(stored, 16 * 2 * NTC)

        @block.gpsimd
        def _(pool):
            made = [0]

            def const(ins):
                made[0] += 1
                ins.then_inc(consts, 1)
                pool.wait_ge(consts, made[0])

            const(pool.memset(ident[:, :], 0.0))
            const(pool.affine_select(out=ident[:, :], in_=ident[:, :], compare_op=ALU.not_equal, fill=1.0,
                                     base=0, pattern=[[-1, 128]], channel_multiplier=1))
            assert made[0] == IDENT

            def load_pair(step):
                for _, i in PREP_AT[step[1]]:
                    h = step[0]
                    until(pool, w_tr, h * WPP + (i + 1 - WPP))
                    pool.dma_start(w_in[:, i, 0, :], gate_pairs[bass.ds(h * WPP + i, 1)].rearrange("a p c -> p (a c)"))\
                        .then_inc(w_here[i], 16)
                    pool.dma_start(w_in[:, i, 1, :].rearrange("p (e c) -> p e c", e=2),
                                   down_pairs[bass.ds(h * WPP + i, 1)].rearrange("a h e c -> h (a e) c"))\
                        .then_inc(w_here[i], 16)

            load_pair((0, 0))
            const(pool.memset(head_mask[:, :], 1.0))
            const(pool.affine_select(out=head_mask[:, :], in_=head_mask[:, :], compare_op=ALU.is_ge, fill=0.0,
                                     base=0, pattern=[[-d, H]], channel_multiplier=1))
            const(pool.affine_select(out=head_mask[:, :], in_=head_mask[:, :], compare_op=ALU.is_ge, fill=0.0,
                                     base=d - 1, pattern=[[d, H]], channel_multiplier=-1))
            const(pool.tensor_copy(ident16[:, :], ident[:, :]))
            for r in range(3):
                const(pool.tensor_copy(stack_mask[32 * r:32 * r + 32, :], head_mask[32 * r:32 * r + 32, 4 * r:4 * r + 4]))
            const(pool.memset(den_pick[:, :], 0.0))
            const(pool.affine_select(out=den_pick[:, :], in_=den_pick[:, :], compare_op=ALU.not_equal, fill=1.0,
                                     base=3 * d, pattern=[[32, 4]], channel_multiplier=-1))
            assert made[0] == MASKS

            def store_pair(step):
                for _, i in PREP_AT[step[1]]:
                    h = step[0]
                    pool.wait_ge(w_hi_done, h * WPP + (i + 1))
                    pool.wait_ge(w_lo_done, h * WPP + (i + 1))
                    pool.dma_start(w_scratch[bass.ds(h * WPP + i, 1)].rearrange("a p b c -> p (a b) c"), w_out[:, i, :, :])\
                        .then_inc(w_stored[i], 16)

            def ones():
                const(pool.memset(v_sb[:, :, :, :, :], 1.0))
                assert made[0] == V_ONES
                const(pool.memset(k_stk[96:97, :, :, :], 1.0))
                assert made[0] == K_ONES
                pool.wait_ge(q_hi_done, NTC)
                pool.wait_ge(q_rows, QROWS)

            def add_constant():
                pool.wait_ge(constant_made, 1)
                pool.wait_ge(ln_sub, 2)
                pool.tensor_tensor(xt[:, :, :], xt[:, :, :], bo_b[:, :].unsqueeze(1).to_broadcast([PT, NP, D]),
                                   ALU.add).then_inc(pre_done, 1)

            pool.wait_ge(q_hi_done, 1)

            def body(step):
                if on(step, 0):
                    h, u = step
                    b = num(step)
                    until(pool, sm_done, (b - 1) * (MT * NCH))
                    pool.tensor_tensor(q_blk[:, u, :, :],
                                       q_hi[:, bass.ds(b * T, T)].unsqueeze(1).to_broadcast([D, H, T]),
                                       head_mask[:, :].unsqueeze(2).to_broadcast([D, H, T]), ALU.mult)\
                        .then_inc(qblk_made, 1)
                if on(step, 1):
                    store_pair(back(step, 1))
                if on(step, -1):
                    load_pair(back(step, -1))
                if on(step, 1):
                    h, u = back(step, 1)
                    b = num((h, u))
                    until(pool, st_done, (b - 1) * (2 * KT))
                    for g in range(HG):
                        last = pool.tensor_tensor(q_st[0:96, u, g, :, :],
                                                  q_stk[0:96, g, bass.ds(b * T, T)].unsqueeze(1).to_broadcast([96, HG, T]),
                                                  stack_mask[:, :].unsqueeze(2).to_broadcast([96, HG, T]), ALU.mult)
                    last.then_inc(qst_made, 1)

            attention(pool, body, B - 2, {1: ones, 2: add_constant})

        @block.scalar
        def _(act):
            def square(n, sq, p0, p1):
                act.wait_ge(ln_sub, n)
                act.activation(sq, xc[:, p0:p1, :], ACT.Square).then_inc(ln_sq, 1)

            def load_root_table(n, sq, some):
                act.activation(sq[:, 0, 0:1], some, ACT.Sqrt).then_inc(table_loaded, 1)
                act.wait_ge(table_loaded, 1 if n == 1 else 2)

            def root(n, p0, p1):
                act.wait_ge(ln_var, n)
                act.activation(stat[:, 3, p0:p1], stat[:, 2, p0:p1], ACT.Sqrt).then_inc(ln_root, 1)

            def query_tokens(c0, c1):
                for c in range(c0, c1):
                    act.wait_ge(xn_tr, c + 1)
                    act.activation(xnT[:, c * TC:(c + 1) * TC], bank[c][:, 0:TC], ACT.Copy).then_inc(xn_cp, 1)

            def queries(c0, c1):
                for c in range(c0, c1):
                    act.wait_ge(q_mm, c + 1)
                    act.activation(q_hi[:, c * TC:(c + 1) * TC], bank[c][:, 0:TC],
                                   ACT.Identity, bias=bqs[:, 0:1], scale=QSCALE).then_inc(q_hi_done, 1)

            act.wait_ge(o_cleared, 2)
            load_root_table(1, sq_first, ones_d[0:PT, 0:1])
            square(1, sq_first, *FIRST)
            for n, w in enumerate((wqT, wk_hi, wv_hi, woT)):
                act.wait_ge(wp_tr, n + 1)
                act.activation(w[:, :], bank[n][:, 0:D], ACT.Copy).then_inc(wp_cp, 1)
            root(1, *FIRST)
            act.wait_ge(bias_in, 16 * 3)
            act.activation(bqs[:, :], bqc[:, :], ACT.Copy, scale=QSCALE).then_inc(bqs_made, 1)
            query_tokens(0, 1)
            act.wait_ge(bqs_made, 1)
            queries(0, 1)

            def gates_and_shared():
                act.wait_ge(small_in, 16 * NSMALL)
                act.activation(tg[:, :], g_raw[:, :], ACT.Tanh).then_inc(gates_made, 1)
                act.wait_ge(cv_mm, 1)
                act.wait_ge(sh_tr, 3)
                act.activation(sg[:, 0, :], SH[:, 0:I], ACT.Copy).then_inc(sh_cp, 1)
                act.activation(sd[:, 0, :], SH[0:I, I:I + D], ACT.Copy).then_inc(sh_cp, 1)
                act.activation(rT[:, :], SH[:, I + D:I + D + E], ACT.Copy).then_inc(sh_cp, 1)
                act.wait_ge(consts, V_ONES)

            def body(step):
                for k in range(KT):
                    j, bt, there = tile_at(step, k, 0)
                    for f in range(2):
                        if there:
                            b = num(bt)
                            act.wait_ge(st_done, b * (2 * KT) + (2 * j + f + 1))
                            if f == 0:
                                until(act, pv_done, b * KT + (j - PR + 1))
                            act.activation(p_exp[0:KP, j % PR, f * 448:(f + 1) * 448], ST[f][0:KP, 0:448],
                                           ACT.Exp).then_inc(exp_done, 1)
                        if f == 0:
                            evacuate(step, k - 1)
                    expert_weights(step, k - 1)
                    if k == 0 and on(step, 2):
                        values(back(step, 2), pj(back(step, 1), "V", NCH - 1), NCH - 1)
                    elif k and k % TPC == 0 and on(step, 1):
                        values(back(step, 1), pj(step, "V", (k - 1) // TPC), (k - 1) // TPC)
                    aside(step, k, (VAR_REST_AT, lambda: square(2, sq_rest, *REST)),
                          (SCALE_REST_AT, lambda: root(2, *REST)), (TOKENS_REST_AT, lambda: query_tokens(1, NTC)),
                          (Q_REST_AT, lambda: queries(1, NTC)),
                          (VAR_AT, lambda: square(3, sq_early, *EARLY)), (SCALE_AT, lambda: root(3, *EARLY)),
                          *((at, lambda c=c: tokens(c)) for at, c in TOKENS_AT.items()),
                          (PROB_AT, lambda: sigmoid(1, *EARLY)),
                          *((at, lambda c=c: weights_out(c)) for at, c in COMBT_AT.items()))

            def tokens(c):
                act.wait_ge(xn_tr, NTC + c + 1)
                if c == 0:
                    act.wait_ge(qblk_made, B)
                act.activation(q_hi[:, c * TC:(c + 1) * TC], TOKB[c][:, 0:TC], ACT.Copy).then_inc(xh_cp, 1)

            def sigmoid(n, p0, p1):
                act.wait_ge(lg_biased, (p1 + 2) // 3)
                act.activation(prob[:, p0:p1, :], prob[:, p0:p1, :], ACT.Sigmoid).then_inc(prob_done, 1)

            def weights_out(c):
                if c == 0:
                    act.wait_ge(qst_made, B)
                for a in range(2):
                    act.wait_ge(cb_tr, 2 * c + a + 1)
                    act.activation(combT[0:EP, a, c * TC:(c + 1) * TC], CTB[2 * c + a][0:EP, 0:TC],
                                   ACT.Copy).then_inc(cb_cp, 1)

            def values(bt, bank_v, c):
                u = bt[1]
                b = num(bt)
                act.wait_ge(vp_done, b * NCH + (c + 1))
                if c == 0:
                    until(act, pv_done, (b - 1) * KT)
                src = bank_v[0:KP, :].rearrange("p (j n) -> p j n", n=D)
                act.activation(v_sb[0:KP, u, c * TPC:(c + 1) * TPC, 0:4, 0:3 * d],
                               src[:, :, 0:12 * d].rearrange("p j (g n) -> p j g n", g=4), ACT.Copy)
                act.activation(v_sb[0:KP, u, c * TPC:(c + 1) * TPC, 4:8, 0:d],
                               src[:, :, 12 * d:16 * d].rearrange("p j (g n) -> p j g n", g=4), ACT.Copy)\
                   .then_inc(v_copied, 1)

            def expert_weights(step, k):
                h, u = step
                for at, i in PREP_AT[u]:
                    if at == k and on(step, 0):
                        act.wait_ge(w_tr, h * WPP + (i + 1))
                        if not isinstance(h, int) or h > 0:
                            act.wait_ge(w_stored[i], h * 16)
                        act.activation(w_out[:, i, 0:4:2, :], EB[:, 0:256].rearrange("p (a b) -> p a b", a=2),
                                       ACT.Copy).then_inc(w_hi_done, 1)

            def evacuate(step, k):
                if k < 0 and on(step, 2):
                    b = num(back(step, 2))
                    act.wait_ge(neg_tr, b + 1)
                    if not (isinstance(b, int) and b == 0):
                        hp, up = back(step, 3)
                        act.wait_ge(row_here[up], hp * 16 + 16)
                    act.activation(neg_row[:, :], EB[0:MT, 0:64].bitcast(fp16), ACT.Copy).then_inc(neg_copied, 1)
                if on(step, 3) and k - 1 == DEN_AT:
                    b = num(back(step, 3))
                    act.wait_ge(rec_done, b + 1)
                    act.activation(rec_wide[:, :, :].rearrange("p a (s r) -> p a s r", r=32),
                                   rec[:, :, :].unsqueeze(3).to_broadcast([PT, 2, 4, 32]), ACT.Copy)\
                       .then_inc(wide_done, 1)
                if k >= 0 and on(step, 0):
                    h, u = step
                    b = num(step)
                    c = k // TPC
                    if k % TPC == 0:
                        act.wait_ge(t_done, b * NCH + (c + 1))
                        act.activation(ctT[:, u, 0, c * CK:(c + 1) * CK], pj(step, "T", c)[:, 0:CK],
                                       ACT.Copy).then_inc(ct_hi, 1)
                    if k % TPC == 2:
                        act.wait_ge(kp_done, b * NCH + (c + 1))
                        if c == 0:
                            until(act, sm_done, (b - 1) * (MT * NCH))
                            if not isinstance(h, int) or h > 0:
                                act.wait_ge(kst_here[u], h * (16 * 3 * HG))
                        act.activation(kparts[:, u, 0, c * CK:(c + 1) * CK], pj(step, "K", c)[:, 0:CK],
                                       ACT.Identity, bias=bkc[:, 0:1]).then_inc(k_hi_done, 1)

            attention(act, body, B, {1: gates_and_shared})

            load_root_table(4, sq_late, stat[:, 2, 0:1])
            square(4, sq_late, *LATE)
            root(4, *LATE)
            tokens(NTC - 1)
            sigmoid(2, *LATE)
            for t in range(NTC):
                act.wait_ge(z_done, t + 1)
                act.activation(h_f[0:I, t, :], ZB[t][0:I, 0:TC], ACT.Silu).then_inc(s_done, 1)
                act.wait_ge(s_done, t + 1)
                act.activation(h_hi[0:I, t, :], h_f[0:I, t, :], ACT.Copy).then_inc(hh_done, 1)
            weights_out(NTC - 1)

            def silu(n, t, first=False):
                m = n * NTC + (NTC + t)
                act.wait_ge(z_done, m + 1)
                if not (first and t < 2):
                    act.wait_ge(h_done, m - (NTC + 1))
                act.activation(s_act[:, t % 2, :], ZB[t][:, 0:TC], ACT.Silu).then_inc(s_done, 1)

            def hi_part(n, t):
                if isinstance(n, int) and n == 0:
                    act.wait_ge(dn_done, t + 1)
                act.wait_ge(h_done, n * NTC + (t + 1))
                act.activation(h_hi[:, t, :], h_f[:, t, :], ACT.Copy).then_inc(hh_done, 1)

            def pairs(base, first=False):
                for q in range(WR):
                    for t in range(NTC):
                        f = first and q == 0
                        silu(base + q, t, f)
                        if t:
                            hi_part(base + q, t - 1)
                        elif not f:
                            hi_part(base + (q - 1), NTC - 1)

            pairs(0, True)
            with act.Fori(1, EP // WR) as i:
                pairs(i * WR)
            hi_part(EP - 1, NTC - 1)
            for c in range(NTC):
                act.wait_ge(dn_done, EP * NTC + (c + 1))
                act.activation(xnT[:, c * TC:(c + 1) * TC], YB[c][:, 0:TC], ACT.Copy).then_inc(y_cp, 1)

        @block.vector
        def _(dve):
            v = nc.vector
            chained = [0]

            def link(ins):
                chained[0] += 1
                ins.then_inc(dve_chain, 1)
                dve.wait_ge(dve_chain, chained[0])

            v.memset(wo_m[:, :, :], 0.0).then_inc(o_cleared, 1)
            v.memset(ones_d[:, :], 1.0).then_inc(o_cleared, 1)

            def centre(p0, p1):
                link(v.reduce_sum(stat[:, 0, p0:p1], xt[:, p0:p1, :], axis=AX.X))
                link(v.tensor_scalar(stat[:, 1, p0:p1], stat[:, 0, p0:p1], -1.0 / D, None, ALU.mult))
                v.tensor_tensor(xc[:, p0:p1, :], xt[:, p0:p1, :],
                                stat[:, 1, p0:p1].unsqueeze(2).to_broadcast([PT, p1 - p0, D]),
                                ALU.add).then_inc(ln_sub, 1)

            def variance(n, sq, p0, p1):
                dve.wait_ge(ln_sq, n)
                link(v.reduce_sum(stat[:, 0, p0:p1], sq, axis=AX.X))
                v.tensor_scalar(stat[:, 2, p0:p1], stat[:, 0, p0:p1], 1.0 / D, EPS_LN, ALU.mult, ALU.add)\
                    .then_inc(ln_var, 1)

            def scale(n, p0, p1):
                dve.wait_ge(ln_root, n)
                link(v.reciprocal(stat[:, 4, p0:p1], stat[:, 3, p0:p1]))
                v.tensor_tensor(xc[:, p0:p1, :], xc[:, p0:p1, :],
                                stat[:, 4, p0:p1].unsqueeze(2).to_broadcast([PT, p1 - p0, D]),
                                ALU.mult).then_inc(ln_done, 1)

            def queries(c0, c1):
                for c in range(c0, c1):
                    dve.wait_ge(q_hi_done, c + 1)
                    if c:
                        dve.wait_ge(q_lo_done, c)
                    link(v.tensor_scalar(q_tmp, bank[c][:, 0:TC], QSCALE, bqs[:, 0:1], ALU.mult, ALU.add))
                    v.tensor_tensor(q_lo[:, c * TC:(c + 1) * TC], q_tmp, q_hi[:, c * TC:(c + 1) * TC],
                                    ALU.subtract).then_inc(q_lo_done, 1)

            dve.wait_ge(x_in, 32)
            centre(*FIRST)
            variance(1, sq_first, *FIRST)
            for n, (lo, hi) in enumerate(((wk_lo, wk_hi), (wv_lo, wv_hi))):
                dve.wait_ge(wp_cp, n + 2)
                v.tensor_tensor(lo[:, :], bank[n + 1][:, 0:D], hi[:, :], ALU.subtract).then_inc(wp_lo, 1)
            scale(1, *FIRST)
            dve.wait_ge(bias_in, 16 * 3)
            dve.wait_ge(bqs_made, 1)
            queries(0, 1)
            dve.wait_ge(o_cleared, 2)
            v.tensor_scalar(bv_rep[:, :], ones_d[:, :], bvc[:, 0:1], None, ALU.mult).then_inc(bv_made, 1)

            def centre_rest():
                dve.wait_ge(x_rest, 32)
                centre(*REST)

            def constant_term():
                dve.wait_ge(small_in, 16 * NSMALL)
                dve.wait_ge(cv_mm, 1)
                dve.wait_ge(sh_cp, 3)
                link(v.tensor_tensor(bo_b[:, :], SH[0:PT, I + D + E:I + 2 * D + E], bo_b[:, :], ALU.add))
                dve.wait_ge(gates_made, 1)
                v.tensor_scalar(bo_b[:, :], bo_b[:, :], tg[:, 0:1], None, ALU.mult).then_inc(constant_made, 1)
                v.tensor_tensor(sg[:, 1, :], SH[:, 0:I], sg[:, 0, :], ALU.subtract).then_inc(sh_lo, 1)
                v.tensor_tensor(sd[:, 1, :], SH[0:I, I:I + D], sd[:, 0, :], ALU.subtract).then_inc(sh_lo, 1)

            def maxima(step, i):
                b = num(back(step, 1))
                if i == 0:
                    until(dve, neg_made, b)
                dve.wait_ge(sm_done, b * (MT * NCH) + (i + 1))
                v.reduce_max(part_max[:, i // NCH, i % NCH:i % NCH + 1], SM[(back(step, 1)[1] + i) % 2][:, 0:CK],
                             axis=AX.X).then_inc(sm_maxed, 1)

            def body(step):
                for k in range(KT):
                    for i in chunks_at(k, 0) if on(step, 1) else []:
                        maxima(step, i)
                    evacuate(step, k - 1)
                    if on(step, 3) and k == LAG:
                        b = num(back(step, 3))
                        dve.wait_ge(pv_done, b * KT + KT)
                        until(dve, nrm_done, b)
                        v.tensor_copy(o_raw[:, :], OB[:, 0:OC]).then_inc(o_copied, 1)
                    for i in chunks_at(k, 1) if on(step, 1) else []:
                        maxima(step, i)
                    expert_weights(step, k - 1)
                    if on(step, 1) and k == NEG_AT - 1:
                        b = num(back(step, 1))
                        dve.wait_ge(sm_maxed, b * (MT * NCH) + MT * NCH)
                        until(dve, neg_tr, b)
                        v.tensor_reduce(neg_max[:, :], part_max[:, :, :], axis=AX.X, op=ALU.max,
                                        negate=True).then_inc(neg_made, 1)
                    aside(step, k, (CENTRE_REST_AT, centre_rest), (VAR_REST_AT, lambda: variance(2, sq_rest, *REST)),
                          (SCALE_REST_AT, lambda: scale(2, *REST)), (Q_REST_AT, lambda: queries(1, NTC)),
                          (CONSTANT_AT, constant_term),
                          (CENTRE_AT, lambda: centre(*EARLY)), (VAR_AT, lambda: variance(3, sq_early, *EARLY)),
                          (SCALE_AT, lambda: scale(3, *EARLY)),
                          *((at, lambda c=c: tokens(c)) for at, c in TOKENS_AT.items()),
                          *((at, lambda g=g: biased(g)) for at, g in LOGITS_AT.items()),
                          (TOP_AT, lambda: largest(1, *EARLY)), (COMB_AT, lambda: router_weights(*EARLY)))

            def tokens(c):
                if c == 0:
                    dve.wait_ge(q_rows, QROWS)
                dve.wait_ge(xh_cp, c + 1)
                cols = slice(c * TC, (c + 1) * TC)
                v.tensor_copy(xnT[:, cols], TOKB[c][:, 0:TC]).then_inc(xf_cp, 1)
                v.tensor_tensor(q_lo[:, cols], TOKB[c][:, 0:TC], q_hi[:, cols], ALU.subtract).then_inc(xl_cp, 1)

            def biased(groups):
                for q in groups:
                    n = min(3, NP - 3 * q)
                    if q == 0:
                        for u in range(2):
                            dve.wait_ge(kst_here[u], (B // 2) * (16 * 3 * HG))
                    dve.wait_ge(lg_mm, q + 1)
                    v.tensor_tensor(prob[:, 3 * q:3 * q + n, :],
                                    LGB[q][0:PT, 0:n * E].rearrange("p (n e) -> p n e", e=E),
                                    eb_b[:, :].unsqueeze(1).to_broadcast([PT, n, E]), ALU.add).then_inc(lg_biased, 1)

            def largest(g, p0, p1):
                dve.wait_ge(prob_done, g)
                for n in range(p0, p1):
                    v.max(top[:, n, :], prob[:, n, :]).then_inc(top_done, 1)
                for n in range(p0, p1):
                    dve.wait_ge(top_done, 2 * p0 + (n - p0 + 1))
                    v.match_replace(comb[:, n, :], top[:, n, :], prob[:, n, :], 0.0).then_inc(top_done, 1)

            def router_weights(p0, p1):
                link(v.reduce_sum(wsum[:, 0, p0:p1], top[:, p0:p1, :], axis=AX.X))
                link(v.tensor_scalar(wsum[:, 1, p0:p1], wsum[:, 0, p0:p1], EPS_TOPK, None, ALU.add))
                link(v.reciprocal(wsum[:, 2, p0:p1], wsum[:, 1, p0:p1]))
                link(v.tensor_scalar(wsum[:, 2, p0:p1], wsum[:, 2, p0:p1], ROUTED_SCALE, None, ALU.mult))
                dve.wait_ge(top_done, 2 * p1)
                link(v.tensor_tensor(comb[:, p0:p1, :], prob[:, p0:p1, :], comb[:, p0:p1, :], ALU.subtract))
                v.tensor_tensor(comb[:, p0:p1, :], comb[:, p0:p1, :],
                                wsum[:, 2, p0:p1].unsqueeze(2).to_broadcast([PT, p1 - p0, E]), ALU.mult)\
                    .then_inc(comb_done, 1)

            def expert_weights(step, k):
                h, u = step
                for at, i in PREP_AT[u]:
                    if at == k and on(step, 0):
                        dve.wait_ge(w_hi_done, h * WPP + (i + 1))
                        v.tensor_tensor(w_out[:, i, 1:4:2, :], EB[:, 0:256].rearrange("p (a b) -> p a b", a=2),
                                        w_out[:, i, 0:4:2, :], ALU.subtract).then_inc(w_lo_done, 1)

            def evacuate(step, k):
                c = k // TPC
                if on(step, 3) and k == OUT_AT and back(step, 3)[1] == 1:
                    h = back(step, 3)[0]
                    dve.wait_ge(op_done, h + 1)
                    if isinstance(h, int) and h == 0:
                        dve.wait_ge(pre_done, 1)
                    v.scalar_tensor_tensor(out=xt[:, bass.ds(h, 1), :], in0=EB[0:PT, 0:D].unsqueeze(1),
                                           scalar=tg[:, 0:1], in1=xt[:, bass.ds(h, 1), :],
                                           op0=ALU.mult, op1=ALU.add).then_inc(x2_done, 1)
                if k >= 0 and on(step, 0):
                    h, u = step
                    b = num(step)
                    if k % TPC == 0:
                        dve.wait_ge(ct_hi, b * NCH + (c + 1))
                        v.tensor_tensor(ctT[:, u, 1, c * CK:(c + 1) * CK], pj(step, "T", c)[:, 0:CK],
                                        ctT[:, u, 0, c * CK:(c + 1) * CK], ALU.subtract).then_inc(ct_lo, 1)
                    if k % TPC == 2:
                        dve.wait_ge(k_hi_done, b * NCH + (c + 1))
                        v.scalar_tensor_tensor(out=kparts[:, u, 1, c * CK:(c + 1) * CK],
                                               in0=pj(step, "K", c)[:, 0:CK], scalar=bkc[:, 0:1],
                                               in1=kparts[:, u, 0, c * CK:(c + 1) * CK],
                                               op0=ALU.add, op1=ALU.subtract).then_inc(k_lo_done, 1)
                if on(step, 3) and k == DEN_AT:
                    b = num(back(step, 3))
                    dve.wait_ge(den_done, b + 1)
                    until(dve, wide_done, b)
                    v.reciprocal(rec[:, :, :], EB[0:PT, 0:8].rearrange("p (a s) -> p a s", a=2)).then_inc(rec_done, 1)
                if on(step, 3) and k == SPREAD_AT:
                    h, u = back(step, 3)
                    b = num((h, u))
                    dve.wait_ge(spread_done, b + 1)
                    if u == 0:
                        until(dve, op_done, h)
                    v.tensor_tensor(o_nrm[:, :, u, :], EB[:, 0:OC].rearrange("p (n t) -> p n t", t=T),
                                    o_raw[:, :].rearrange("p (n t) -> p n t", t=T), ALU.mult).then_inc(nrm_done, 1)

            attention(dve, body)

            dve.wait_ge(x2_done, NP)
            centre(*LATE)
            variance(4, sq_late, *LATE)
            scale(4, *LATE)
            tokens(NTC - 1)
            biased((4, 5))
            largest(2, *LATE)
            router_weights(*LATE)

            for t in range(NTC):
                dve.wait_ge(hh_done, t + 1)
                v.tensor_tensor(h_lo[0:I, t, :], h_f[0:I, t, :], h_hi[0:I, t, :], ALU.subtract).then_inc(hl_done, 1)

            def weigh(i, q, t, first=False):
                n = i * WR + q
                m = n * NTC + (NTC + t)
                dve.wait_ge(s_done, m + 1)
                if first and q == 0:
                    dve.wait_ge(hl_done, t + 1)
                if first:
                    if t == 0:
                        dve.wait_ge(c_here[q], 32)
                    if t == NTC - 1:
                        dve.wait_ge(c_here[q], 64)
                elif t == 0:
                    dve.wait_ge(c_here[q], i * 32 + 64)
                dve.wait_ge(hh_done, m - (NTC - 1))
                v.tensor_tensor(h_f[:, t, :], c_ring[q][:, t * TC:(t + 1) * TC], s_act[:, t % 2, :], ALU.mult).then_inc(h_done, 1)

            def lo_part(n, t):
                if isinstance(n, int) and n == 0:
                    dve.wait_ge(dn_done, t + 1)
                dve.wait_ge(hh_done, n * NTC + (NTC + t + 1))
                v.tensor_tensor(h_lo[:, t, :], h_f[:, t, :], h_hi[:, t, :], ALU.subtract).then_inc(hl_done, 1)

            def pairs(i, first=False):
                base = i * WR
                for q in range(WR):
                    for t in range(NTC):
                        weigh(i, q, t, first)
                        if t:
                            lo_part(base + q, t - 1)
                        elif not (first and q == 0):
                            lo_part(base + (q - 1), NTC - 1)

            pairs(0, True)
            with dve.Fori(1, EP // WR) as i:
                pairs(i)
            lo_part(EP - 1, NTC - 1)
            for c in range(NTC):
                dve.wait_ge(y_tr, c + 1)
                v.scalar_tensor_tensor(out=xc[:, c * PPC:(c + 1) * PPC, :],
                                       in0=bank[4 + c][0:PT, :].rearrange("p (n c) -> p n c", c=D),
                                       scalar=tg[:, 1:2], in1=xt[:, c * PPC:(c + 1) * PPC, :],
                                       op0=ALU.mult, op1=ALU.add).then_inc(fin_done, 1)

        @block.tensor
        def _(pe):
            pe.wait_ge(consts, IDENT)
            pe.wait_ge(weights_in, 16 * 4)
            for n in range(4):
                pe.transpose(bank[n][:, 0:D], w_raw[:, n, :], ident[:, :]).then_inc(wp_tr, 1)

            def transpose_tokens(c, bank_c):
                for i in range(PPC):
                    last = pe.transpose(bank_c[:, i * PT:(i + 1) * PT], xc[:, c * PPC + i, :], ident[0:PT, 0:PT])
                last.then_inc(xn_tr, 1)

            pe.wait_ge(wp_cp, 4)
            pe.wait_ge(wp_lo, 2)
            def query_tokens(n, c0, c1):
                pe.wait_ge(ln_done, n)
                for c in range(c0, c1):
                    transpose_tokens(c, bank[c])

            def queries(c0, c1):
                for c in range(c0, c1):
                    pe.wait_ge(xn_cp, c + 1)
                    pe.matmul(bank[c][:, 0:TC], wqT[:, :], xnT[:, c * TC:(c + 1) * TC], start=True, stop=True)\
                      .then_inc(q_mm, 1)

            query_tokens(1, 0, 1)
            queries(0, 1)

            def shared_and_router():
                pe.wait_ge(late_in, 16 * 3)
                pe.transpose(SH[:, 0:I], sh_raw[0:I, 0, :], ident[0:I, 0:I]).then_inc(sh_tr, 1)
                pe.transpose(SH[0:I, I:I + D], sh_raw[:, 1, 0:I], ident[:, :]).then_inc(sh_tr, 1)
                for a in range(2):
                    last = pe.transpose(SH[:, I + D + a * (E // 2):I + D + (a + 1) * (E // 2)], r_raw[:, a, :],
                                        ident[0:E // 2, 0:E // 2])
                last.then_inc(sh_tr, 1)
                pe.wait_ge(bv_made, 1)
                pe.matmul(SH[0:PT, I + D + E:I + 2 * D + E], bv_rep[:, :], woT[:, :], start=True, stop=True)\
                  .then_inc(cv_mm, 1)
                pe.wait_ge(q_hi_done, NTC)
                pe.wait_ge(q_lo_done, NTC)
                pe.wait_ge(consts, MASKS)

            def bank_free():
                pe.wait_ge(consts, K_ONES)
                pe.wait_ge(sh_cp, 3)
                pe.wait_ge(sh_lo, 2)
                pe.wait_ge(constant_made, 1)
                pe.wait_ge(wo_rows, 16 * H)

            def value_product(bt, j):
                h, u = bt
                b = num(bt)
                pe.wait_ge(exp_done, b * (2 * KT) + (2 * j + 2))
                if j % TPC == 0:
                    pe.wait_ge(v_copied, b * NCH + (j // TPC + 1))
                if j == 0:
                    until(pe, o_copied, b)
                for g in range(VG):
                    at, w = (0, VC) if g < 4 else (VC, T)
                    src = VC * g if g < 4 else 4 * VC + T * (g - 4)
                    last = pe.matmul(OB[32 * (g % 4):32 * (g % 4) + 32, at:at + w],
                                     v_sb[0:KP, u, j, g, :], p_exp[0:KP, j % PR, src:src + w],
                                     start=(j == 0 and g < 4), stop=(j == KT - 1), skip_group_check=True)
                last.then_inc(pv_done, 1)

            def scores(bt, j, f):
                h, u = bt
                b = num(bt)
                if j == 0 and f == 0:
                    pe.wait_ge(kst_here[u], h * (16 * 3 * HG) + 16 * 3 * HG)
                    pe.wait_ge(row_here[u], h * 16 + 16)
                until(pe, exp_done, b * (2 * KT) + (2 * j + f - 1))
                for g in (2 * f, 2 * f + 1):
                    last = pe.matmul(ST[f][0:KP, (g % 2) * GC:(g % 2 + 1) * GC],
                                     k_stk[0:97, u, g, j * KP:(j + 1) * KP],
                                     q_st[0:97, u, g, :, :].rearrange("p a t -> p (a t)"), start=True, stop=True)
                last.then_inc(st_done, 1)

            def maxima(step, i):
                u = back(step, 1)[1]
                b = num(back(step, 1))
                m, c = i // NCH, i % NCH
                if i == 0:
                    pe.wait_ge(qblk_made, b + 1)
                    pe.wait_ge(k_hi_done, b * NCH + NCH)
                until(pe, sm_maxed, b * (MT * NCH) + (i - 1))
                rows = q_blk[:, u, :, :].rearrange("p a t -> p (a t)")[:, 128 * m:128 * m + 128]
                pe.matmul(SM[(u + i) % 2][:, 0:CK], rows, kparts[:, u, 0, c * CK:(c + 1) * CK],
                          start=True, stop=True).then_inc(sm_done, 1)

            def body(step):
                for k in range(KT):
                    js, bs, scores_there = tile_at(step, k, 0)
                    jv, bv_, values_there = tile_at(step, k, 1)
                    for f in range(2):
                        if scores_there:
                            scores(bs, js, f)
                        for i in chunks_at(k, 0) if f == 0 and on(step, 1) else []:
                            maxima(step, i)
                    if values_there:
                        value_product(bv_, jv)
                    for i in chunks_at(k, 1) if on(step, 1) else []:
                        maxima(step, i)
                    c = k // TPC
                    if on(step, 0):
                        h, u = step
                        b = num(step)
                        if k % TPC == 0:
                            if c == 0:
                                pe.wait_ge(ctx_here[u], h * 16 + 16)
                            until(pe, k_hi_done, b * NCH + c)
                            until(pe, k_lo_done, b * NCH + c)
                            for i in range(TPC):
                                last = pe.transpose(pj(step, "T", c)[:, i * KP:(i + 1) * KP],
                                                    ctx_in[:, u, c * TPC + i, :], ident[0:KP, 0:KP])
                            last.then_inc(t_done, 1)
                        if k % TPC == 2:
                            pe.wait_ge(ct_lo, b * NCH + (c + 1))
                            until(pe, v_copied, (b - 1) * NCH + c)
                            for i, (w, part) in enumerate(((wk_hi, 0), (wk_lo, 0), (wk_hi, 1))):
                                last = pe.matmul(pj(step, "K", c)[:, 0:CK], w[:, :],
                                                 ctT[:, u, part, c * CK:(c + 1) * CK], start=(i == 0), stop=(i == 2))
                            last.then_inc(kp_done, 1)
                    if on(step, 1) and k % TPC == 3:
                        u = back(step, 1)[1]
                        b = num(back(step, 1))
                        if on(step, 0):
                            pe.wait_ge(ct_lo, (b + 1) * NCH + (c + 1))
                        else:
                            pe.wait_ge(k_lo_done, (b + 1) * NCH)
                            pe.wait_ge(v_copied, b * NCH + c)
                        for i in range(TPC):
                            cols = slice((c * TPC + i) * KP, (c * TPC + i + 1) * KP)
                            for n, (part, w) in enumerate(((0, wv_hi), (0, wv_lo), (1, wv_hi))):
                                last = pe.matmul(pj(step, "V", c)[0:KP, i * D:(i + 1) * D], ctT[:, u, part, cols],
                                                 w[:, :], start=(n == 0), stop=(n == 2))
                        last.then_inc(vp_done, 1)
                    if on(step, 0):
                        h, u = step
                        for n, (at, i) in enumerate(PREP_AT[u]):
                            if at == k:
                                pe.wait_ge(w_here[i], h * 32 + 32)
                                until(pe, w_lo_done, h * WPP + i)
                                if n == 0:
                                    until(pe, neg_copied, num(back(step, 1)))
                                if at > SPREAD_AT and on(step, 3):
                                    pe.wait_ge(nrm_done, num(back(step, 3)) + 1)
                                for a in range(2):
                                    last = pe.transpose(EB[:, a * 128:(a + 1) * 128], w_in[:, i, a, :], ident[:, :])
                                last.then_inc(w_tr, 1)
                    if on(step, 3) and k == DEN_AT:
                        b = num(back(step, 3))
                        if on(step, 0):
                            done = [i for at, i in PREP_AT[step[1]] if at < DEN_AT][-1]
                            pe.wait_ge(w_lo_done, step[0] * WPP + (done + 1))
                        else:
                            pe.wait_ge(neg_copied, min(num(back(step, 1)), B))
                            pe.wait_ge(w_lo_done, EP)
                            pe.wait_ge(x2_done, b // 2)
                        pe.wait_ge(o_copied, b + 1)
                        for a in range(2):
                            last = pe.matmul(EB[0:PT, 4 * a:4 * a + 4], o_raw[:, a * PT:(a + 1) * PT], den_pick[:, :],
                                             start=True, stop=True)
                        last.then_inc(den_done, 1)
                    if on(step, 3) and k == SPREAD_AT:
                        pe.wait_ge(wide_done, num(back(step, 3)) + 1)
                        for a in range(2):
                            last = pe.matmul(EB[:, a * PT:(a + 1) * PT], rec_wide[:, a, :], ident[0:PT, 0:PT],
                                             start=True, stop=True)
                        last.then_inc(spread_done, 1)
                    if on(step, 3) and k == OUT_AT and back(step, 3)[1] == 1:
                        h = back(step, 3)[0]
                        if on(step, 0):
                            pe.wait_ge(w_lo_done, step[0] * WPP + (PREP_AT[step[1]][-1][1] + 1))
                        pe.wait_ge(nrm_done, h * 2 + 2)
                        for n in range(4):
                            last = pe.matmul(EB[0:PT, 0:D], o_nrm[:, n, :, :].rearrange("p a t -> p (a t)"),
                                             wo_m[:, n, :], start=(n == 0), stop=(n == 3))
                        last.then_inc(op_done, 1)
                    if on(step, 1) and k == NEG_AT:
                        b = num(back(step, 1))
                        if on(step, 0):
                            pe.wait_ge(w_lo_done, step[0] * WPP + (PREP_AT[step[1]][-1][1] + 1))
                        if on(step, 3):
                            pe.wait_ge(nrm_done, num(back(step, 3)) + 1)
                            if back(step, 3)[1] == 1:
                                pe.wait_ge(x2_done, back(step, 3)[0] + 1)
                        pe.wait_ge(neg_made, b + 1)
                        pe.transpose(EB[0:MT, 0:64].bitcast(fp16), neg_max[:, :], ident16[:, :]).then_inc(neg_tr, 1)
                    aside(step, k, (TOKENS_REST_AT, lambda: query_tokens(2, 1, NTC)),
                          (Q_REST_AT, lambda: queries(1, NTC)), (BANK_FREE_AT, bank_free),
                          *((at, lambda c=c: tokens(c)) for at, c in TOKENS_AT.items()),
                          *((at, lambda g=g: logits(g)) for at, g in LOGITS_AT.items()),
                          *((at, lambda c=c: weights_out(c)) for at, c in COMBT_AT.items()))

            def tokens(c):
                if c == 0:
                    pe.wait_ge(ln_done, 3)
                    pe.wait_ge(v_copied, (B - 1) * NCH)
                elif c == 1:
                    pe.wait_ge(v_copied, (B - 1) * NCH + 2)
                elif c == 2:
                    pe.wait_ge(xl_cp, 2)
                else:
                    pe.wait_ge(ln_done, 4)
                    pe.wait_ge(cb_cp, 5)
                transpose_tokens(c, TOKB[c])

            def logits(groups):
                for q in groups:
                    n = min(3, NP - 3 * q)
                    pe.wait_ge(xf_cp, (3 * q + n - 1) // PPC + 1)
                    if q == 0:
                        pe.wait_ge(sm_maxed, B * (MT * NCH))
                    elif q == 2:
                        pe.wait_ge(v_copied, B * NCH)
                    elif q == 3:
                        pe.wait_ge(xl_cp, 3)
                    elif q == 4:
                        pe.wait_ge(cb_cp, 6)
                    for i in range(n):
                        last = pe.matmul(LGB[q][0:PT, i * E:(i + 1) * E],
                                         xnT[:, (3 * q + i) * PT:(3 * q + i + 1) * PT], rT[:, :], start=True, stop=True)
                    last.then_inc(lg_mm, 1)

            def weights_out(c):
                pe.wait_ge(comb_done, 1 if c < 3 else 2)
                if c == 0:
                    pe.wait_ge(lg_biased, 4)
                elif c == 2:
                    pe.wait_ge(cb_cp, 2)
                elif c == 3:
                    pe.wait_ge(xl_cp, NTC)
                for a in range(2):
                    for i in range(PPC):
                        last = pe.transpose(CTB[2 * c + a][0:EP, i * PT:(i + 1) * PT],
                                            comb[:, c * PPC + i, :].rearrange("p (m a) -> p a m", a=2)[:, a, :],
                                            ident[0:PT, 0:PT])
                    last.then_inc(cb_tr, 1)

            attention(pe, body, B, {1: shared_and_router})

            hilo = ((0, 0), (1, 0), (0, 1))
            xparts = (q_hi, q_lo)
            hparts = (h_hi, h_lo)
            def shared_up(t):
                for i, (a, b) in enumerate(hilo):
                    last = pe.matmul(ZB[t][0:I, 0:TC], sg[:, a, :], xparts[b][:, t * TC:(t + 1) * TC],
                                     start=(i == 0), stop=(i == 2))
                last.then_inc(z_done, 1)

            def up(m, t, q):
                pe.wait_ge(s_done, m - (NTC - 1))
                for j, (a, b) in enumerate(hilo):
                    last = pe.matmul(ZB[t][:, 0:TC], w_ring[:, q, a, :], xparts[b][:, t * TC:(t + 1) * TC],
                                     start=(j == 0), stop=(j == 2))
                last.then_inc(z_done, 1)

            pe.wait_ge(xl_cp, NTC - 1)
            pe.wait_ge(cb_cp, 4)
            for t in range(NTC - 1):
                shared_up(t)
            pe.wait_ge(x2_done, NP)
            tokens(NTC - 1)
            logits((4, 5))
            pe.wait_ge(xl_cp, NTC)
            shared_up(NTC - 1)
            pe.wait_ge(ring_here[0], 16)
            for t in range(NTC - 1):
                up(NTC + t, t, 0)
            weights_out(NTC - 1)
            up(NTC + (NTC - 1), NTC - 1, 0)
            pe.wait_ge(cb_cp, 2 * NTC)
            pe.wait_ge(lg_biased, 6)

            def down(n, t, q, shared=False, end=False):
                pe.wait_ge(hl_done, n * NTC + (NTC + t + 1))
                for i, (a, b) in enumerate(hilo):
                    rows = slice(0, I if shared else 128)
                    w = sd[:, a, :] if shared else w_ring[:, q, 2 + a, :]
                    last = pe.matmul(YB[t][:, 0:TC], w, hparts[b][rows, t, :], start=(shared and i == 0),
                                     stop=(end and i == 2), skip_group_check=True)
                last.then_inc(dn_done, 1)

            def pairs(i, first=False):
                for q in range(WR):
                    n = i * WR + q
                    for t in range(NTC):
                        m = n * NTC + (NTC + t)
                        down(n - 1, t, (q - 1) % WR, shared=first and q == 0)
                        if first and q == 0:
                            continue
                        if t == 0:
                            pe.wait_ge(ring_here[q], i * 16 + 16)
                        up(m, t, q)

            pairs(0, True)
            with pe.Fori(1, EP // WR) as i:
                pairs(i)
            def finish(c):
                pe.wait_ge(y_cp, c + 1)
                for i in range(PPC):
                    last = pe.transpose(bank[4 + c][0:PT, i * D:(i + 1) * D],
                                        xnT[:, (c * PPC + i) * PT:(c * PPC + i + 1) * PT], ident[:, :])
                last.then_inc(y_tr, 1)

            for t in range(NTC):
                down(EP - 1, t, WR - 1, end=True)
                if t:
                    finish(t - 1)
            finish(NTC - 1)


_INS = ['x', 'ctx_1024', 'g_xattn', 'g_ffn', 'L0_xattn_Wq', 'L0_xattn_bq', 'L0_xattn_Wk', 'L0_xattn_bk',
        'L0_xattn_Wv', 'L0_xattn_bv', 'L0_xattn_Wo', 'L0_xattn_bo', 'L0_ffn_router_w', 'L0_ffn_expert_bias',
        'L0_ffn_w_gate', 'L0_ffn_w_down', 'L0_ffn_w_gate_shared', 'L0_ffn_w_down_shared']
_OUTS = [((32, 56, 128), 'float32')]


def kernel(**inputs):
    import numpy as _np
    import concourse.bacc as _bacc
    from concourse import mybir as _mybir
    from concourse.bass_utils import run_bass_kernel_spmd as _run

    nc = _bacc.Bacc("TRN2", target_bir_lowering=False, num_devices=1)
    arrays, args = {}, []
    for name in _INS:
        a = _np.ascontiguousarray(inputs[name])
        arrays[f"in_{name}_dram"] = a
        args.append(nc.dram_tensor(f"in_{name}_dram", a.shape, _mybir.dt.from_np(a.dtype), kind="ExternalInput").ap())
    for i, (shape, dtype) in enumerate(_OUTS):
        dt = _mybir.dt.from_np(_np.dtype(dtype))
        args.append(nc.dram_tensor(f"out_{i}_dram", shape, dt, kind="ExternalOutput").ap())
    flamingo_gated_block(nc, *args)
    r = _run(nc, [arrays], core_ids=[0])
    got = tuple(r.results[0][f"out_{i}_dram"] for i in range(len(_OUTS)))
    return got[0]
```
